# Optimizing a Trainium2 kernel written in Bass

```python
import numpy as np
import jax
import jax.numpy as jnp

def _softmax(x, axis=-1):
    return jax.nn.softmax(x, axis=axis)

def _gelu(x):
    return jax.nn.gelu(x, approximate=True)

def _silu(x):
    return jax.nn.silu(x)

def _sigmoid(x):
    return jax.nn.sigmoid(x)

def _layernorm(x, axis=-1, eps=1e-05):
    m = jnp.mean(x, axis=axis, keepdims=True)
    v = jnp.var(x, axis=axis, keepdims=True)
    return (x - m) / jnp.sqrt(v + eps)

def _scatter_add(tgt, idx, src, axis=0):
    return tgt.at[idx].add(src)

def _segment_sum(src, seg, n):
    return jax.ops.segment_sum(src, seg, n)
kernel_name = 'mk_prb_d1_jaxref_r4_8797f0'

def setup_inputs(seed: int=0):
    np.random.seed(seed)
    _w = jnp.asarray

    def _L0_attn_setup():
        import jax, jax.numpy as jnp
        import numpy as np
        B, T, D_MODEL, D_SSM = (8, 512, 256, 256)
        key = jax.random.key(seed)
        ks = jax.random.split(key, 7)
        sc_in = 1.0 / np.sqrt(D_MODEL)
        sc_ssm = 1.0 / np.sqrt(D_SSM)
        return {'x': jax.random.normal(ks[0], (B, T, D_MODEL), dtype=jnp.float32), 'Wp': jax.random.uniform(ks[1], (D_MODEL, 3 * D_SSM), jnp.float32, -sc_in, sc_in), 'bp': jax.random.uniform(ks[2], (3 * D_SSM,), jnp.float32, -sc_in, sc_in), 'Wu': jax.random.uniform(ks[3], (D_MODEL, D_SSM), jnp.float32, -sc_in, sc_in), 'bu': jax.random.uniform(ks[4], (D_SSM,), jnp.float32, -sc_in, sc_in), 'Wo': jax.random.uniform(ks[5], (D_SSM, D_MODEL), jnp.float32, -sc_ssm, sc_ssm), 'bo': jax.random.uniform(ks[6], (D_MODEL,), jnp.float32, -sc_ssm, sc_ssm)}
    _L0_attn_in = _L0_attn_setup()

    def _L0_ffn_setup():
        import jax, jax.numpy as jnp
        import numpy as np
        from jax import lax
        DIM = 256
        INTER = 128
        N_EXPERTS = 16
        TOPK = 4
        ROUTE_SCALE = 2.5
        VOCAB = 8000

        def _silu_and_mul(gu):
            gate, up = jnp.split(gu, 2, axis=-1)
            return jax.nn.silu(gate) * up
        key = jax.random.key(seed)
        ks = jax.random.split(key, 8)
        x = jax.random.normal(ks[0], (2, 128, DIM), dtype=jnp.float32)
        input_ids = jax.random.randint(ks[1], (2, 128), 0, VOCAB)
        s = 0.02
        gate_w = jax.random.normal(ks[2], (N_EXPERTS, DIM), dtype=jnp.float32) * s
        gate_b = jax.random.normal(ks[3], (N_EXPERTS,), dtype=jnp.float32) * s
        w13 = jax.random.normal(ks[4], (N_EXPERTS, 2 * INTER, DIM), dtype=jnp.float32) * s
        w2 = jax.random.normal(ks[5], (N_EXPERTS, DIM, INTER), dtype=jnp.float32) * s
        w13_s = jax.random.normal(ks[6], (2 * INTER, DIM), dtype=jnp.float32) * s
        w2_s = jax.random.normal(ks[7], (DIM, INTER), dtype=jnp.float32) * s
        return {'x': x, 'input_ids': input_ids, 'gate_w': gate_w, 'gate_b': gate_b, 'w13': w13, 'w2': w2, 'w13_s': w13_s, 'w2_s': w2_s}
    _L0_ffn_in = _L0_ffn_setup()
    _d = {'L0_attn_x': _L0_attn_in['x'], 'L0_attn_Wp': _L0_attn_in['Wp'], 'L0_attn_bp': _L0_attn_in['bp'], 'L0_attn_Wu': _L0_attn_in['Wu'], 'L0_attn_bu': _L0_attn_in['bu'], 'L0_attn_Wo': _L0_attn_in['Wo'], 'L0_attn_bo': _L0_attn_in['bo'], 'L0_ffn_input_ids': _L0_ffn_in['input_ids'], 'L0_ffn_gate_w': _L0_ffn_in['gate_w'], 'L0_ffn_gate_b': _L0_ffn_in['gate_b'], 'L0_ffn_w13': _L0_ffn_in['w13'], 'L0_ffn_w2': _L0_ffn_in['w2'], 'L0_ffn_w13_s': _L0_ffn_in['w13_s'], 'L0_ffn_w2_s': _L0_ffn_in['w2_s']}
    _x0 = _d['L0_attn_x']
    _d['L0_attn_x'] = jax.random.normal(jax.random.fold_in(jax.random.key(seed), 1), (8, 1024, 256), dtype=_x0.dtype)
    del _x0
    return _d

def reference(L0_attn_x, L0_attn_Wp, L0_attn_bp, L0_attn_Wu, L0_attn_bu, L0_attn_Wo, L0_attn_bo, L0_ffn_input_ids, L0_ffn_gate_w, L0_ffn_gate_b, L0_ffn_w13, L0_ffn_w2, L0_ffn_w13_s, L0_ffn_w2_s):

    def _L0_attn_ref(x, Wp, bp, Wu, bu, Wo, bo):
        import jax, jax.numpy as jnp
        import numpy as np
        B, T, D_MODEL, D_SSM = (8, 512, 256, 256)
        Bb, Tt, _ = x.shape
        d_ssm = Wu.shape[1]
        params = x @ Wp + bp
        params = params.reshape(Bb, Tt, 3, d_ssm)
        u = x @ Wu + bu
        w = params[:, :, 0]
        k = params[:, :, 1]

        def step(s, inp):
            w_t, k_t, u_t = inp
            gate = jax.nn.sigmoid(w_t)
            s = gate * (s * jnp.tanh(k_t) + u_t) + (1.0 - gate) * s
            return (s, s)
        s0 = jnp.zeros((Bb, d_ssm), dtype=x.dtype)
        xs = (w.transpose(1, 0, 2), k.transpose(1, 0, 2), u.transpose(1, 0, 2))
        _, ys = jax.lax.scan(step, s0, xs)
        y = ys.transpose(1, 0, 2)
        return y @ Wo + bo

    def _L0_ffn_ref(x, input_ids, gate_w, gate_b, w13, w2, w13_s, w2_s):
        import jax, jax.numpy as jnp
        import numpy as np
        from jax import lax
        DIM = 256
        INTER = 128
        N_EXPERTS = 16
        TOPK = 4
        ROUTE_SCALE = 2.5
        VOCAB = 8000

        def _silu_and_mul(gu):
            gate, up = jnp.split(gu, 2, axis=-1)
            return jax.nn.silu(gate) * up
        B, S, D = x.shape
        xt = x.reshape(-1, D)
        T = xt.shape[0]
        scores = jax.nn.sigmoid(xt.astype(jnp.float32) @ gate_w.T)
        biased = scores + gate_b
        _, idx = lax.top_k(biased, TOPK)
        w = jnp.take_along_axis(scores, idx, axis=-1)
        w = w / jnp.sum(w, axis=-1, keepdims=True)
        w = w * ROUTE_SCALE
        comb = jnp.zeros((T, N_EXPERTS), jnp.float32)
        comb = comb.at[jnp.arange(T)[:, None], idx].add(w)
        comb = comb.astype(x.dtype)

        def expert_body(y, args):
            w13_e, w2_e, c_e = args
            h = _silu_and_mul(xt @ w13_e.T)
            return (y + c_e[:, None] * (h @ w2_e.T), None)
        y, _ = lax.scan(expert_body, jnp.zeros_like(xt), (w13, w2, comb.T))
        y = y + _silu_and_mul(xt @ w13_s.T) @ w2_s.T
        return y.astype(x.dtype).reshape(B, S, D)
    x = L0_attn_x
    xn = _layernorm(x, axis=-1)
    x = x + _L0_attn_ref(xn, L0_attn_Wp, L0_attn_bp, L0_attn_Wu, L0_attn_bu, L0_attn_Wo, L0_attn_bo) + _L0_ffn_ref(xn, L0_ffn_input_ids, L0_ffn_gate_w, L0_ffn_gate_b, L0_ffn_w13, L0_ffn_w2, L0_ffn_w13_s, L0_ffn_w2_s)
    return x

_drawn_inputs = setup_inputs


def setup_inputs(seed=0):
    import zlib

    import numpy as np

    out = dict(_drawn_inputs(seed))
    spreads = {}
    factors = {'L0_attn_bp': 8.0,
     'L0_attn_bu': 2.723,
     'L0_ffn_gate_w': 4.584,
     'L0_ffn_gate_b': 8.0,
     'L0_ffn_w13': 3.868,
     'L0_ffn_w2': 3.86,
     'L0_ffn_w13_s': 4.845,
     'L0_ffn_w2_s': 4.84,
     'L0_attn_bo': 3.394}
    for name, (base, spread) in spreads.items():
        noise = np.random.default_rng([zlib.crc32(name.encode()), seed]).standard_normal(out[name].shape)
        drawn = base * np.exp(spread * noise) if base else spread * noise
        out[name] = jnp.asarray(drawn.astype(out[name].dtype))
    for name, factor in factors.items():
        out[name] = (out[name] * factor).astype(out[name].dtype)
    return out
```

```python
from contextlib import ExitStack

import concourse.bass as bass
from concourse import mybir

F32 = mybir.dt.float32
F16 = mybir.dt.float16
ALU = mybir.AluOpType
ACT = mybir.ActivationFunctionType
AX_X = mybir.AxisListType.X

P = 128
TILE = 512
SUB = TILE // P
TOPK = 4
ROUTE_SCALE = 2.5
EPS = 1e-5
WSCALE = 64.0
UNSCALE = 1.0 / WSCALE
ABSENT = -3.0e38
PADS = 4
STAGES = 5
AHEAD = 4
RING = 4
LAG = 2

SLOT_STATS, SLOT_NORM, SLOT_TURN, SLOT_SPLIT, SLOT_ROUTE, SLOT_MASK, SLOT_COMB = 6, 7, 9, 9, 11, 12, 14


def scan_moe_kernel(nc, x, attn_w, attn_b, bo, gate_b, expert_w, out):
    tokens, D = x.shape
    KC = D // P
    E = gate_b.shape[1]
    NE = E + 1
    I = (expert_w.shape[2] - D) // (2 * KC)
    TILES = tokens // TILE
    PER_SEQ = 2
    SEQS = TILES // PER_SEQ
    assert I == P and KC == 2 and TILES % PER_SEQ == 0

    x_tiles = x.rearrange("(t s p) d -> t p s d", s=SUB, p=P)
    out_tiles = out.rearrange("(t s p) d -> t p s d", s=SUB, p=P)

    with ExitStack() as ctx:
        def sb(name, shape, dt=F32):
            return ctx.enter_context(nc.sbuf_tensor(name, shape, dt))

        def sem(name):
            return ctx.enter_context(nc.semaphore(name))

        AW = 3 * D + D + E
        attn_f = sb("attn_f", [P, KC, AW])
        attn_hi = sb("attn_hi", [P, KC, AW], F16)
        attn_lo = sb("attn_lo", [P, KC, AW], F16)
        WO, RT = 3 * D, 4 * D
        EW = 2 * I * KC + D
        stage = sb("stage", [P, STAGES, EW])
        exp_hi = sb("exp_hi", [P, NE, EW], F16)
        exp_lo = sb("exp_lo", [P, NE, EW], F16)
        DOWN = 2 * I * KC
        bias = sb("bias", [P, 3, KC])
        half_bw = sb("half_bw", [P, KC])
        bo_bc = sb("bo_bc", [P, 1, D])
        gate_b_bc = sb("gate_b_bc", [P, 1, E])
        ident = sb("ident", [P, P])
        credit = sb("credit", [P, 5])
        minus_half = sb("minus_half", [P, SUB])

        xs = sb("xs", [P, 2, SUB, D])
        xn = sb("xn", [P, SUB, D])
        x_hi = sb("x_hi", [P, 2, KC, TILE], F16)
        x_lo = sb("x_lo", [P, 2, KC, TILE], F16)
        stats = sb("stats", [P, SUB, 6])
        mv = sb("mv", [P, SUB, 2])
        var_eps = sb("var_eps", [P, SUB])
        seed = sb("seed", [P, SUB])
        n1 = sb("n1", [P, SUB])
        n2 = sb("n2", [P, SUB])
        rstd = sb("rstd", [P, SUB])
        half_tanh = sb("half_tanh", [P, SUB, E])
        score = sb("score", [P, SUB, E])
        biased = sb("biased", [P, SUB, E + PADS])
        top8 = sb("top8", [P, SUB, 8])
        cut = sb("cut", [P, SUB, E + PADS])
        chosen = sb("chosen", [P, SUB, E])
        picked = sb("picked", [P, SUB, E])
        total = sb("total", [P, SUB])
        inv_total = sb("inv_total", [P, SUB])
        comb = sb("comb", [P, SUB, E])
        comb_t = sb("comb_t", [E, TILE])
        comb_row = sb("comb_row", [1, E, TILE])
        comb_bc = sb("comb_bc", [P, RING, TILE])
        tanh_w = sb("tanh_w", [P, KC, TILE])
        tanh_k = sb("tanh_k", [P, KC, TILE])
        u = sb("u", [P, KC, TILE])
        gate = sb("gate", [P, TILE])
        decay_1 = sb("decay_1", [P, TILE])
        decay = sb("decay", [P, TILE])
        drive = sb("drive", [P, TILE])
        state = sb("state", [P, KC, 2, TILE])
        s_hi = sb("s_hi", [P, KC, TILE], F16)
        s_lo = sb("s_lo", [P, KC, TILE], F16)
        silu = sb("silu", [P, 2, TILE])
        act = sb("act", [P, 2, TILE])
        act_c = sb("act_c", [P, 2, TILE])
        h_hi = sb("h_hi", [P, 2, TILE], F16)
        h_lo = sb("h_lo", [P, 2, TILE], F16)
        y = sb("y", [P, 2, SUB, D])

        acc = ctx.enter_context(nc.psum_tensor("acc", [P, SUB, D], F32))
        gate_up = ctx.enter_context(nc.psum_tensor("gate_up", [P, 2, 2, TILE], F32))
        misc = ctx.enter_context(nc.psum_tensor("misc", [P, 2, TILE], F32))

        attn_landed = sem("attn_landed")
        small_landed = sem("small_landed")
        stage_landed = [sem(f"stage_landed{i}") for i in range(STAGES)]
        x_landed = [sem(f"x_landed{i}") for i in range(2)]
        ident_ready = sem("ident_ready")
        half_ready = sem("half_ready")
        const_ready = sem("const_ready")
        attn_hi_ready = sem("attn_hi_ready")
        attn_lo_ready = sem("attn_lo_ready")
        exp_hi_ready = sem("exp_hi_ready")
        exp_lo_ready = sem("exp_lo_ready")
        stats_done = sem("stats_done")
        moments_done = sem("moments_done")
        var_ready = sem("var_ready")
        seed_ready = sem("seed_ready")
        newton = sem("newton")
        xn_ready = sem("xn_ready")
        resid_ready = sem("resid_ready")
        turned = sem("turned")
        x_hi_ready = sem("x_hi_ready")
        x_lo_ready = sem("x_lo_ready")
        logits_full = sem("logits_full")
        logits_taken = sem("logits_taken")
        route = sem("route")
        comb_turned = sem("comb_turned")
        comb_t_ready = sem("comb_t_ready")
        comb_row_landed = sem("comb_row_landed")
        comb_bc_ready = sem("comb_bc_ready")
        comb_bc_free = sem("comb_bc_free")
        proj_full = sem("proj_full")
        proj_taken = sem("proj_taken")
        scan_step = sem("scan_step")
        up_full = sem("up_full")
        silu_ready = sem("silu_ready")
        up_free = sem("up_free")
        h_hi_ready = sem("h_hi_ready")
        h_lo_ready = sem("h_lo_ready")
        h_free = sem("h_free")
        acc_free = sem("acc_free")
        y_free = [sem(f"y_free{i}") for i in range(2)]

        dve_passed = sem("dve_passed")
        pool_passed = sem("pool_passed")
        sp_passed = sem("sp_passed")

        ROUTE_STEPS = 2 + SUB + 1 + SUB + 5
        SCAN_STEPS = 7
        HALVES = 2

        block = ctx.enter_context(nc.Block())

        def tiles(eng, body):
            for par in range(PER_SEQ):
                body(0, par, False)
            with eng.Fori(1, SEQS - 1) as q:
                for par in range(PER_SEQ):
                    body(q, par, False)
            for par in range(PER_SEQ):
                body(SEQS - 1, par, par == PER_SEQ - 1)

        def count(q, par, per_tile, k):
            return q * (PER_SEQ * per_tile) + (par * per_tile + k)

        def ep(par, e):
            return (par * NE + e) % 2

        @block.sync
        def _(sp):
            sp.dma_start(xs[:, 0], x_tiles[0]).then_inc(x_landed[0], 16)
            sp.dma_start(attn_f[:], attn_w).then_inc(attn_landed, 16)
            for e in range(NE):
                if e >= STAGES:
                    sp.wait_ge(exp_lo_ready, e - STAGES + 1)
                sp.dma_start(stage[:, e % STAGES], expert_w[e]).then_inc(stage_landed[e % STAGES], 16)
                if e == STAGES - 1:
                    sp.dma_start(xs[:, 1], x_tiles[1]).then_inc(x_landed[1], 16)
                    sp.wait_ge(comb_t_ready, 1)
                    sp.dma_start(comb_row[0:1, :, :], comb_t[:, :]).then_inc(comb_row_landed, 16)

            def step(q, par, last):
                if not last:
                    sp.wait_ge(comb_t_ready, count(q, par, 1, 2))
                    sp.sem_inc(sp_passed, 1)
                    sp.wait_ge(comb_bc_ready, count(q, par, E, E))
                    sp.sem_inc(sp_passed, 1)
                    sp.dma_start(comb_row[0:1, :, :], comb_t[:, :]).then_inc(comb_row_landed, 16)
                sp.wait_ge(acc_free, count(q, par, HALVES, 2 * HALVES))
                sp.sem_inc(sp_passed, 1)
                sp.dma_start(out_tiles[q * PER_SEQ + par], y[:, par]).then_inc(y_free[par], 16)

            def load(q, par):
                sp.dma_start(xs[:, par], x_tiles[(q + 1) * PER_SEQ + par]).then_inc(x_landed[par], 16)

            with sp.Fori(0, SEQS - 1) as q:
                for par in range(PER_SEQ):
                    step(q, par, False)
                    load(q, par)
            for par in range(PER_SEQ):
                step(SEQS - 1, par, par == PER_SEQ - 1)
            for par in range(PER_SEQ):
                sp.wait_ge(y_free[par], 16 * (SEQS + 1))

        @block.gpsimd
        def _(pool):
            pool.memset(ident[:], 0.0).then_inc(ident_ready, 1)
            pool.memset(minus_half[:], -0.5).then_inc(half_ready, 1)
            pool.wait_ge(ident_ready, 1)
            pool.affine_select(out=ident[:], in_=ident[:], compare_op=ALU.not_equal, fill=1.0, base=0,
                               pattern=[[-1, P]], channel_multiplier=1).then_inc(ident_ready, 1)
            pool.wait_ge(half_ready, 1)

            def root_seed(q, par):
                pool.wait_ge(var_ready, count(q, par, 1, 1))
                pool.tensor_tensor(seed[:], var_eps[:], minus_half[:], ALU.pow).then_inc(seed_ready, 1)

            def residual(q, par):
                pool.wait_ge(xn_ready, count(q, par, SUB, SUB))
                pool.tensor_tensor(xs[:, par], xs[:, par], bo_bc[:, :, :].to_broadcast([P, SUB, D]),
                                   ALU.add).then_inc(resid_ready, 1)

            def step(q, par, last):
                pool.wait_ge(comb_row_landed, count(q, par, 16, 16))
                for e in range(E):
                    pool.wait_ge(comb_bc_free, count(q, par, E, e + 1))
                    pool.sem_inc(pool_passed, 1)
                    pool.partition_broadcast(comb_bc[:, e % RING], comb_row[0:1, e, :], P).then_inc(comb_bc_ready, 1)
                    if not last and e == SLOT_STATS + RING - 1:
                        root_seed(q + (par == 1), 1 - par)
                    if not last and e == SLOT_NORM + RING:
                        residual(q + (par == 1), 1 - par)

            pool.wait_ge(small_landed, 48)
            root_seed(0, 0)
            residual(0, 0)
            tiles(pool, step)

        @block.scalar
        def _(act_e):
            act_e.dma_start(bias[:], attn_b).then_inc(small_landed, 16)
            act_e.dma_start(bo_bc[:, 0, :], bo.to_broadcast([P, D])).then_inc(small_landed, 16)
            act_e.dma_start(gate_b_bc[:, 0, :], gate_b.to_broadcast([P, E])).then_inc(small_landed, 16)

            def split_x(q, par, buf):
                for c in range(KC):
                    act_e.wait_ge(turned, count(q, par, KC, c + 1))
                    act_e.activation(x_hi[:, buf, c], misc[:, c], ACT.Copy).then_inc(x_hi_ready, 1)

            def split_expert(e):
                act_e.wait_ge(stage_landed[e % STAGES], 16 * (e // STAGES + 1))
                act_e.activation(exp_hi[:, e], stage[:, e % STAGES], ACT.Copy, scale=WSCALE).then_inc(exp_hi_ready, 1)

            def logits(q, par):
                act_e.wait_ge(logits_full, count(q, par, 1, 1))
                act_e.activation(half_tanh[:], misc[:, 0, 0:SUB * E].rearrange("p (s e) -> p s e", e=E), ACT.Tanh,
                                 scale=0.5 * UNSCALE).then_inc(logits_taken, 1)

            def comb_out(q, par):
                act_e.wait_ge(comb_turned, count(q, par, 1, 1))
                if not (isinstance(q, int) and q == par == 0):
                    act_e.wait_ge(comb_row_landed, count(q, par, 16, 0))
                act_e.activation(comb_t[:, :], misc[0:E, 1], ACT.Copy).then_inc(comb_t_ready, 1)

            def step(q, par, last):
                for i, (dst, fn, scale, b) in enumerate(
                        [(tanh_w, ACT.Tanh, 0.5 * UNSCALE, half_bw)] * KC + [(tanh_k, ACT.Tanh, UNSCALE, bias[:, 1])] * KC
                        + [(u, ACT.Identity, UNSCALE, bias[:, 2])] * KC):
                    c = i % KC
                    act_e.wait_ge(proj_full, count(q, par, 3 * KC, i + 1))
                    act_e.activation(dst[:, c], misc[:, c], fn, scale=scale, bias=b[:, c:c + 1]).then_inc(proj_taken, 1)
                for e in range(NE):
                    n = ep(par, e)
                    act_e.wait_ge(up_full, count(q, par, NE, e + 1))
                    act_e.activation(silu[:, n], gate_up[:, n, 0], ACT.Silu, scale=UNSCALE).then_inc(silu_ready, 1)
                    if e < E:
                        act_e.wait_ge(comb_bc_free, count(q, par, E, RING + e + 1))
                    else:
                        act_e.wait_ge(up_free, count(q, par, NE, e + 3))
                    act_e.wait_ge(h_free, count(q, par, NE, e + 1))
                    act_e.activation(h_hi[:, n], act_c[:, n], ACT.Copy).then_inc(h_hi_ready, 1)
                    if isinstance(q, int) and q == par == 0 and e + AHEAD < NE:
                        split_expert(e + AHEAD)
                    if not last:
                        nq, npar = q + (par == 1), 1 - par
                        if e == SLOT_TURN:
                            split_x(nq, npar, npar)
                        if e == SLOT_ROUTE:
                            logits(nq, npar)
                        if e == SLOT_COMB:
                            comb_out(nq, npar)

            act_e.wait_ge(attn_landed, 16)
            act_e.activation(attn_hi[:], attn_f[:], ACT.Copy, scale=WSCALE).then_inc(attn_hi_ready, 1)
            split_x(0, 0, 0)
            logits(0, 0)
            for e in range(AHEAD):
                split_expert(e)
            comb_out(0, 0)
            act_e.wait_ge(const_ready, 1)
            tiles(act_e, step)

        @block.vector
        def _(dve):
            def norm_stats(q, par):
                dve.wait_ge(x_landed[par], q * 16 + 16)
                for s in range(SUB):
                    dve.bn_stats(stats[:, s], xs[:, par, s]).then_inc(stats_done, 1)

            def norm_rstd(q, par):
                for s in range(SUB):
                    dve.wait_ge(stats_done, count(q, par, SUB, s + 1))
                    dve.sem_inc(dve_passed, 1)
                    dve.bn_aggr(mv[:, s], stats[:, s]).then_inc(moments_done, 1)
                dve.wait_ge(moments_done, count(q, par, SUB, SUB))
                dve.tensor_scalar(var_eps[:], mv[:, :, 1], EPS, None, ALU.add).then_inc(var_ready, 1)

            def norm(q, par):
                dve.wait_ge(seed_ready, count(q, par, 1, 1))
                dve.tensor_tensor(n1[:], seed[:], seed[:], ALU.mult).then_inc(newton, 1)
                dve.wait_ge(newton, count(q, par, 4, 1))
                dve.tensor_tensor(n2[:], n1[:], var_eps[:], ALU.mult).then_inc(newton, 1)
                dve.wait_ge(newton, count(q, par, 4, 2))
                dve.tensor_scalar(n1[:], n2[:], -0.5, 1.5, ALU.mult, ALU.add).then_inc(newton, 1)
                dve.wait_ge(newton, count(q, par, 4, 3))
                dve.tensor_tensor(rstd[:], n1[:], seed[:], ALU.mult).then_inc(newton, 1)
                dve.wait_ge(newton, count(q, par, 4, 4))
                for s in range(SUB):
                    dve.tensor_scalar(xn[:, s], xs[:, par, s], mv[:, s, 0:1], rstd[:, s:s + 1],
                                      ALU.subtract, ALU.mult).then_inc(xn_ready, 1)

            def split_expert(e):
                dve.wait_ge(exp_hi_ready, e + 1)
                dve.scalar_tensor_tensor(out=exp_lo[:, e], in0=stage[:, e % STAGES], scalar=WSCALE, in1=exp_hi[:, e],
                                         op0=ALU.mult, op1=ALU.subtract).then_inc(exp_lo_ready, 1)

            def split_x(q, par, buf):
                for c in range(KC):
                    dve.wait_ge(x_hi_ready, count(q, par, KC, c + 1))
                    dve.tensor_tensor(x_lo[:, buf, c], misc[:, c], x_hi[:, buf, c], ALU.subtract).then_inc(x_lo_ready, 1)

            def mask(q, par):
                k = 0

                def done(ins):
                    nonlocal k
                    k += 1
                    ins.then_inc(route, 1)

                def ready():
                    dve.wait_ge(route, count(q, par, ROUTE_STEPS, k))

                dve.wait_ge(logits_taken, count(q, par, 1, 1))
                done(dve.tensor_scalar(score[:], half_tanh[:], 0.5, 0.5, ALU.mult, ALU.add))
                ready()
                done(dve.tensor_tensor(biased[:, :, 0:E], score[:], gate_b_bc[:, :, :].to_broadcast([P, SUB, E]), ALU.add))
                ready()
                dve.sem_inc(dve_passed, 1)
                for s in range(SUB):
                    done(dve.max(top8[:, s], biased[:, s]))
                ready()
                done(dve.memset(top8[:, :, TOPK:8], ABSENT))
                ready()
                dve.sem_inc(dve_passed, 1)
                for s in range(SUB):
                    done(dve.match_replace(cut[:, s], top8[:, s], biased[:, s], -2.0e38))
                ready()
                return k

            def weigh(q, par, k):
                def done(ins):
                    nonlocal k
                    k += 1
                    ins.then_inc(route, 1)
                    dve.wait_ge(route, count(q, par, ROUTE_STEPS, k))

                done(dve.tensor_tensor(chosen[:], cut[:, :, 0:E], biased[:, :, 0:E], ALU.not_equal))
                done(dve.tensor_tensor(picked[:], chosen[:], score[:], ALU.mult))
                done(dve.tensor_reduce(total[:], picked[:], AX_X, ALU.add))
                done(dve.reciprocal(inv_total[:], total[:]))
                done(dve.scalar_tensor_tensor(
                    out=comb[:], in0=picked[:], scalar=ROUTE_SCALE,
                    in1=inv_total[:, :].unsqueeze(2).to_broadcast([P, SUB, E]), op0=ALU.mult, op1=ALU.mult))
                assert k == ROUTE_STEPS

            def scan_part(q, par, part):
                c, part = divmod(part, 3)
                k = c * SCAN_STEPS

                def ready(i):
                    dve.wait_ge(scan_step, count(q, par, KC * SCAN_STEPS, k + i))

                if part == 0:
                    dve.wait_ge(proj_taken, count(q, par, 3 * KC, 3 * KC))
                    dve.tensor_scalar(gate[:], tanh_w[:, c], 0.5, 0.5, ALU.mult, ALU.add).then_inc(scan_step, 1)
                    ready(1)
                    dve.scalar_tensor_tensor(out=decay_1[:], in0=tanh_k[:, c], scalar=-1.0, in1=gate[:],
                                             op0=ALU.add, op1=ALU.mult).then_inc(scan_step, 1)
                    ready(2)
                    dve.tensor_scalar(decay[:], decay_1[:], 1.0, None, ALU.add).then_inc(scan_step, 1)
                elif part == 1:
                    dve.tensor_tensor(drive[:], gate[:], u[:, c], ALU.mult).then_inc(scan_step, 1)
                    ready(4)
                    first = 0.0 if par == 0 else state[:, c, 0, TILE - 1:TILE]
                    dve.tensor_tensor_scan(state[:, c, par], decay[:], drive[:], first,
                                           ALU.mult, ALU.add).then_inc(scan_step, 1)
                else:
                    ready(5)
                    dve.tensor_copy(s_hi[:, c], state[:, c, par]).then_inc(scan_step, 1)
                    ready(6)
                    dve.tensor_tensor(s_lo[:, c], state[:, c, par], s_hi[:, c], ALU.subtract).then_inc(scan_step, 1)

            def step(q, par, last):
                nq, npar = q + (par == 1), 1 - par
                steps = 0
                for e in range(NE):
                    n = ep(par, e)
                    dve.wait_ge(silu_ready, count(q, par, NE, e + 1))
                    dst = act if e < E else act_c
                    dve.scalar_tensor_tensor(out=dst[:, n], in0=gate_up[:, n, 1], scalar=UNSCALE, in1=silu[:, n],
                                             op0=ALU.mult, op1=ALU.mult).then_inc(up_free, 1)
                    if e < E:
                        dve.wait_ge(comb_bc_ready, count(q, par, E, e + 1))
                        dve.wait_ge(up_free, count(q, par, NE, e + 3))
                        dve.tensor_tensor(act_c[:, n], act[:, n], comb_bc[:, e % RING], ALU.mult).then_inc(comb_bc_free, 1)
                    dve.wait_ge(h_hi_ready, count(q, par, NE, e + 1))
                    dve.tensor_tensor(h_lo[:, n], act_c[:, n], h_hi[:, n], ALU.subtract).then_inc(h_lo_ready, 1)
                    if isinstance(q, int) and q == par == 0 and e + AHEAD < NE:
                        split_expert(e + AHEAD)
                    if e < 3 * KC:
                        scan_part(q, par, e)
                    if last:
                        continue
                    if e == SLOT_STATS:
                        norm_stats(nq, npar)
                        norm_rstd(nq, npar)
                    if e == SLOT_NORM:
                        norm(nq, npar)
                    if e == SLOT_SPLIT:
                        split_x(nq, npar, npar)
                    if e == SLOT_ROUTE:
                        steps = mask(nq, npar)
                    if e == SLOT_MASK:
                        weigh(nq, npar, steps)
                dve.wait_ge(h_free, count(q, par, NE, NE + 2))
                dve.wait_ge(resid_ready, count(q, par, 1, 1))
                dve.wait_ge(y_free[par], q * 16 + 16)
                w = SUB // HALVES
                for b in range(HALVES):
                    dve.scalar_tensor_tensor(out=y[:, par, b * w:(b + 1) * w], in0=acc[:, b * w:(b + 1) * w], scalar=UNSCALE,
                                             in1=xs[:, par, b * w:(b + 1) * w], op0=ALU.mult, op1=ALU.add).then_inc(acc_free, 1)

            dve.memset(biased[:, :, E:E + PADS], ABSENT).then_inc(up_free, 2)
            dve.memset(credit[:, 0:1], 0.0).then_inc(acc_free, HALVES)
            dve.memset(credit[:, 1:2], 0.0).then_inc(h_free, 2)
            dve.memset(credit[:, 2:3], 0.0).then_inc(comb_bc_free, RING)
            for i in range(2):
                dve.memset(credit[:, 3 + i:4 + i], 0.0).then_inc(y_free[i], 16)
            norm_stats(0, 0)
            norm_rstd(0, 0)
            norm(0, 0)
            dve.wait_ge(small_landed, 48)
            dve.tensor_scalar(half_bw[:], bias[:, 0], 0.5, None, ALU.mult).then_inc(const_ready, 1)
            dve.wait_ge(attn_hi_ready, 1)
            dve.scalar_tensor_tensor(out=attn_lo[:], in0=attn_f[:], scalar=WSCALE, in1=attn_hi[:],
                                     op0=ALU.mult, op1=ALU.subtract).then_inc(attn_lo_ready, 1)
            split_x(0, 0, 0)
            dve.wait_ge(up_free, 2)
            weigh(0, 0, mask(0, 0))
            for e in range(AHEAD):
                split_expert(e)
            tiles(dve, step)

        @block.tensor
        def _(pe):
            def turn(q, par):
                for c in range(KC):
                    for s in range(SUB):
                        pe.wait_ge(xn_ready, count(q, par, SUB, s + 1))
                        last = pe.transpose(misc[:, c, s * P:(s + 1) * P], xn[:, s, c * P:(c + 1) * P], ident[:])
                    last.then_inc(turned, 1)

            def router(q, par, buf):
                pe.wait_ge(x_lo_ready, count(q, par, KC, KC))
                for s in range(SUB):
                    terms = [(xp, wp, c) for c in range(KC) for xp, wp in
                             ((x_hi, attn_hi), (x_hi, attn_lo), (x_lo, attn_hi), (x_lo, attn_lo))]
                    for i, (xp, wp, c) in enumerate(terms):
                        last = pe.matmul(misc[:, 0, s * E:(s + 1) * E], xp[:, buf, c, s * P:(s + 1) * P],
                                         wp[:, c, RT:RT + E], start=(i == 0), stop=(i == len(terms) - 1))
                last.then_inc(logits_full, 1)

            def turn_comb(q, par):
                pe.wait_ge(route, count(q, par, ROUTE_STEPS, ROUTE_STEPS))
                for s in range(SUB):
                    last = pe.transpose(misc[0:E, 1, s * P:(s + 1) * P], comb[:, s], ident[:])
                last.then_inc(comb_turned, 1)

            def product(dst, w_hi, w_lo, x_h, x_l):
                for c in range(KC):
                    pe.matmul(dst, w_hi(c), x_h(c), start=(c == 0), stop=False)
                    pe.matmul(dst, w_hi(c), x_l(c), start=False, stop=False)
                    last = pe.matmul(dst, w_lo(c), x_h(c), start=False, stop=(c == KC - 1))
                return last

            def project(q, par):
                for i in range(3 * KC):
                    if i == 0:
                        pe.wait_ge(logits_taken, count(q, par, 1, 1))
                    elif i == 1:
                        pe.wait_ge(comb_t_ready, count(q, par, 1, 1))
                    else:
                        pe.wait_ge(proj_taken, count(q, par, 3 * KC, i - 1))
                    product(misc[:, i % 2], lambda c: attn_hi[:, c, i * P:(i + 1) * P], lambda c: attn_lo[:, c, i * P:(i + 1) * P],
                            lambda c: x_hi[:, par, c], lambda c: x_lo[:, par, c]).then_inc(proj_full, 1)

            def up(q, par, e):
                n = ep(par, e)
                pe.wait_ge(up_free, count(q, par, NE, e + 1))
                for g in range(2):
                    last = product(gate_up[:, n, g],
                                   lambda c: exp_hi[:, e, c * 2 * I + g * I:c * 2 * I + (g + 1) * I],
                                   lambda c: exp_lo[:, e, c * 2 * I + g * I:c * 2 * I + (g + 1) * I],
                                   lambda c: x_hi[:, par, c], lambda c: x_lo[:, par, c])
                last.then_inc(up_full, 1)

            def add_to_acc(v_hi, v_lo, w_hi, w_lo, first=False, end=False):
                for s in range(SUB):
                    cols = slice(s * P, (s + 1) * P)
                    for i, (v, w) in enumerate(((v_hi, w_hi), (v_hi, w_lo), (v_lo, w_hi))):
                        last = pe.matmul(acc[:, s], v[:, cols], w, start=(first and i == 0 and s % 2 == 0),
                                         stop=(end and i == 2), skip_group_check=True)
                return last

            def down(q, par, e, end=False):
                n = ep(par, e)
                if e == 0:
                    pe.wait_ge(acc_free, count(q, par, HALVES, HALVES))
                pe.wait_ge(h_hi_ready, count(q, par, NE, e + 1))
                pe.wait_ge(h_lo_ready, count(q, par, NE, e + 1))
                last = add_to_acc(h_hi[:, n], h_lo[:, n], exp_hi[:, e, DOWN:DOWN + D], exp_lo[:, e, DOWN:DOWN + D],
                                  first=(e == 0), end=end)
                last.then_inc(h_free, 1)

            def recurrence_out(q, par):
                pe.wait_ge(scan_step, count(q, par, KC * SCAN_STEPS, KC * SCAN_STEPS))
                for c in range(KC):
                    add_to_acc(s_hi[:, c], s_lo[:, c], attn_hi[:, c, WO:WO + D], attn_lo[:, c, WO:WO + D])

            def step(q, par, last):
                nq, npar = q + (par == 1), 1 - par
                project(q, par)
                for e in range(NE):
                    if isinstance(q, int) and q == par == 0:
                        pe.wait_ge(exp_lo_ready, e + 1)
                    up(q, par, e)
                    if e >= LAG:
                        down(q, par, e - LAG)
                    if last:
                        continue
                    if e == SLOT_TURN:
                        pe.wait_ge(proj_taken, count(q, par, 3 * KC, 3 * KC))
                        turn(nq, npar)
                    if e == SLOT_ROUTE:
                        router(nq, npar, npar)
                    if e == SLOT_COMB:
                        turn_comb(nq, npar)
                recurrence_out(q, par)
                down(q, par, NE - 2)
                down(q, par, NE - 1, end=True)

            pe.wait_ge(ident_ready, 2)
            turn(0, 0)
            pe.wait_ge(attn_lo_ready, 1)
            router(0, 0, 0)
            turn_comb(0, 0)
            tiles(pe, step)


_OUTS = [((8, 1024, 256), 'float32')]


def kernel(L0_attn_x, L0_attn_Wp, L0_attn_bp, L0_attn_Wu, L0_attn_bu, L0_attn_Wo, L0_attn_bo, L0_ffn_input_ids,
           L0_ffn_gate_w, L0_ffn_gate_b, L0_ffn_w13, L0_ffn_w2, L0_ffn_w13_s, L0_ffn_w2_s):
    import numpy as np
    import concourse.bacc as bacc
    from concourse.bass_utils import run_bass_kernel_spmd

    def chunks(w):
        w = np.asarray(w)
        return w.reshape(w.shape[0] // P, P, w.shape[1]).transpose(1, 0, 2)

    x = np.asarray(L0_attn_x)
    d = x.shape[-1]
    attn_w = np.concatenate([chunks(np.asarray(L0_attn_Wp)[:, :2 * d]), chunks(L0_attn_Wu), chunks(L0_attn_Wo),
                             chunks(np.asarray(L0_ffn_gate_w).T)], axis=2)
    attn_b = np.concatenate([np.asarray(L0_attn_bp)[:2 * d], np.asarray(L0_attn_bu)]).reshape(3, d // P, P).transpose(2, 0, 1)
    w13 = np.concatenate([np.asarray(L0_ffn_w13), np.asarray(L0_ffn_w13_s)[None]])
    w2 = np.concatenate([np.asarray(L0_ffn_w2), np.asarray(L0_ffn_w2_s)[None]])
    ne, two_i, _ = w13.shape
    up = w13.transpose(0, 2, 1).reshape(ne, d // P, P, two_i).transpose(0, 2, 1, 3).reshape(ne, P, -1)
    expert_w = np.concatenate([up, w2.transpose(0, 2, 1)], axis=2)
    arrays = {
        "x": x.reshape(-1, d), "attn_w": attn_w, "attn_b": attn_b, "bo": np.asarray(L0_attn_bo)[None],
        "gate_b": np.asarray(L0_ffn_gate_b)[None], "expert_w": expert_w,
    }
    nc = bacc.Bacc("TRN2", target_bir_lowering=False, num_devices=1)
    args = []
    for name in arrays:
        arrays[name] = np.ascontiguousarray(arrays[name])
        args.append(nc.dram_tensor(name, arrays[name].shape, mybir.dt.from_np(arrays[name].dtype), kind="ExternalInput").ap())
    out = nc.dram_tensor("out", arrays["x"].shape, F32, kind="ExternalOutput").ap()
    scan_moe_kernel(nc, *args, out)
    r = run_bass_kernel_spmd(nc, [arrays], core_ids=[0])
    return r.results[0]["out"].reshape(x.shape)
```

```python
from contextlib import ExitStack

import concourse.bass as bass
from concourse import mybir

F32 = mybir.dt.float32
F16 = mybir.dt.float16
ALU = mybir.AluOpType
ACT = mybir.ActivationFunctionType
AX_X = mybir.AxisListType.X

P = 128
TILE = 512
SUB = TILE // P
TOPK = 4
ROUTE_SCALE = 2.5
EPS = 1e-5
WSCALE = 64.0
UNSCALE = 1.0 / WSCALE
ABSENT = -3.0e38
PADS = 4
QUADS = 4
STAGES = 12
AHEAD = (6, 14)
RING = 4
LAG = 2

SLOT_STATS, SLOT_MOMENTS, SLOT_NORM, SLOT_TURN, SLOT_ROUTE, SLOT_TANH, SLOT_WEIGH, SLOT_COMB = 2, 3, 4, 6, 8, 9, 10, 12
SLOT_SCAN = (0, 1, 5, 7, 11, 13)


def scan_moe_kernel(nc, x, attn_w, attn_b, bo, gate_b, expert_w, out):
    tokens, D = x.shape
    KC = D // P
    E = gate_b.shape[1]
    NE = E + 1
    I = (expert_w.shape[2] - D) // (2 * KC)
    TILES = tokens // TILE
    PER_SEQ = 2
    SEQS = TILES // PER_SEQ
    assert I == P and KC == 2 and TILES % PER_SEQ == 0

    x_tiles = x.rearrange("(t s p) d -> t p s d", s=SUB, p=P)
    out_tiles = out.rearrange("(t s p) d -> t p s d", s=SUB, p=P)

    with ExitStack() as ctx:
        def sb(name, shape, dt=F32):
            return ctx.enter_context(nc.sbuf_tensor(name, shape, dt))

        def sem(name):
            return ctx.enter_context(nc.semaphore(name))

        AW = 3 * D + D + E
        attn_f = sb("attn_f", [P, KC, AW])
        attn_hi = sb("attn_hi", [P, KC, 4 * D], F16)
        attn_lo = sb("attn_lo", [P, KC, 4 * D], F16)
        WO, RT = 3 * D, 4 * D
        EW = 2 * I * KC + D
        stage = sb("stage", [P, STAGES, EW])
        exp_hi = sb("exp_hi", [P, NE, EW], F16)
        exp_lo = sb("exp_lo", [P, NE, EW], F16)
        DOWN = 2 * I * KC
        bias = sb("bias", [P, 3, KC])
        half_bw = sb("half_bw", [P, KC])
        bo_bc = sb("bo_bc", [P, 1, D])
        gate_b_bc = sb("gate_b_bc", [P, 1, E])
        ident = sb("ident", [P, P])
        credit = sb("credit", [P, 5])
        minus_half = sb("minus_half", [P, SUB])

        xs = sb("xs", [P, 2, SUB, D])
        xn = sb("xn", [P, SUB, D])
        x_hi = sb("x_hi", [P, 2, KC, TILE], F16)
        x_lo = sb("x_lo", [P, 2, KC, TILE], F16)
        stats = sb("stats", [P, SUB, 6])
        mv = sb("mv", [P, SUB, 2])
        var_eps = sb("var_eps", [P, SUB])
        seed = sb("seed", [P, SUB])
        n1 = sb("n1", [P, SUB])
        n2 = sb("n2", [P, SUB])
        rstd = sb("rstd", [P, SUB])
        router_w = sb("router_w", [P, KC, 2, E], F16)
        logits = sb("logits", [P, SUB, E])
        half_tanh = sb("half_tanh", [P, SUB, E])
        score = sb("score", [P, SUB, E])
        biased = sb("biased", [P, SUB, E + PADS])
        top8 = sb("top8", [P, SUB, 8])
        cut = sb("cut", [P, SUB, E + PADS])
        chosen = sb("chosen", [P, SUB, E])
        picked = sb("picked", [P, SUB, E])
        total = sb("total", [P, SUB])
        inv_total = sb("inv_total", [P, SUB])
        comb = sb("comb", [P, SUB, E])
        comb_t = sb("comb_t", [E, TILE])
        comb_row = sb("comb_row", [P, E // QUADS, TILE])
        comb_bc = sb("comb_bc", [P, RING, TILE])
        tanh_w = sb("tanh_w", [P, KC, TILE])
        tanh_k = sb("tanh_k", [P, KC, TILE])
        u = sb("u", [P, KC, TILE])
        gate = sb("gate", [P, TILE])
        decay_1 = sb("decay_1", [P, TILE])
        decay = sb("decay", [P, TILE])
        drive = sb("drive", [P, TILE])
        state = sb("state", [P, KC, 2, TILE])
        s_hi = sb("s_hi", [P, KC, TILE], F16)
        s_lo = sb("s_lo", [P, KC, TILE], F16)
        silu = sb("silu", [P, 2, TILE])
        act = sb("act", [P, 2, TILE])
        act_c = sb("act_c", [P, 2, TILE])
        h_hi = sb("h_hi", [P, 2, TILE], F16)
        h_lo = sb("h_lo", [P, 2, TILE], F16)
        y = sb("y", [P, 2, SUB, D])

        acc = ctx.enter_context(nc.psum_tensor("acc", [P, SUB, D], F32))
        gate_up = ctx.enter_context(nc.psum_tensor("gate_up", [P, 2, 2, TILE], F32))
        misc = ctx.enter_context(nc.psum_tensor("misc", [P, 2, TILE], F32))

        attn_landed = sem("attn_landed")
        small_landed = sem("small_landed")
        stage_landed = [sem(f"stage_landed{i}") for i in range(STAGES)]
        x_landed = [sem(f"x_landed{i}") for i in range(2)]
        ident_ready = sem("ident_ready")
        half_ready = sem("half_ready")
        const_ready = sem("const_ready")
        attn_hi_ready = sem("attn_hi_ready")
        attn_lo_ready = sem("attn_lo_ready")
        exp_hi_ready = sem("exp_hi_ready")
        exp_lo_ready = sem("exp_lo_ready")
        stats_done = sem("stats_done")
        moments_done = sem("moments_done")
        var_ready = sem("var_ready")
        seed_ready = sem("seed_ready")
        newton = sem("newton")
        xn_ready = sem("xn_ready")
        resid_ready = sem("resid_ready")
        turned = sem("turned")
        x_hi_ready = sem("x_hi_ready")
        x_lo_ready = sem("x_lo_ready")
        logits_full = sem("logits_full")
        logits_taken = sem("logits_taken")
        squashed = sem("squashed")
        route = sem("route")
        comb_turned = sem("comb_turned")
        comb_t_ready = sem("comb_t_ready")
        comb_row_landed = sem("comb_row_landed")
        comb_bc_ready = sem("comb_bc_ready")
        comb_bc_free = sem("comb_bc_free")
        proj_full = sem("proj_full")
        proj_taken = sem("proj_taken")
        scan_step = sem("scan_step")
        up_full = sem("up_full")
        silu_ready = sem("silu_ready")
        up_free = sem("up_free")
        h_hi_ready = sem("h_hi_ready")
        h_lo_ready = sem("h_lo_ready")
        h_free = sem("h_free")
        acc_free = sem("acc_free")
        y_free = [sem(f"y_free{i}") for i in range(2)]

        dve_passed = sem("dve_passed")
        pool_passed = sem("pool_passed")
        sp_passed = sem("sp_passed")

        ROUTE_STEPS = 2 + SUB + 1 + SUB + 5
        SCAN_STEPS = 7
        HALVES = 2

        block = ctx.enter_context(nc.Block())

        def tiles(eng, body):
            for par in range(PER_SEQ):
                body(0, par, False)
            with eng.Fori(1, SEQS - 1) as q:
                for par in range(PER_SEQ):
                    body(q, par, False)
            for par in range(PER_SEQ):
                body(SEQS - 1, par, par == PER_SEQ - 1)

        def count(q, par, per_tile, k):
            return q * (PER_SEQ * per_tile) + (par * per_tile + k)

        def is_first(q, par):
            return isinstance(q, int) and q == 0 and par == 0

        def ep(par, e):
            return (par * NE + e) % 2

        @block.sync
        def _(sp):
            sp.dma_start(xs[:, 0], x_tiles[0]).then_inc(x_landed[0], 16)
            sp.dma_start(attn_f[:], attn_w).then_inc(attn_landed, 16)
            for e in range(NE):
                if e >= STAGES:
                    sp.wait_ge(exp_lo_ready, e - STAGES + 1)
                sp.dma_start(stage[:, e % STAGES], expert_w[e]).then_inc(stage_landed[e % STAGES], 16)
                if e == STAGES - 1:
                    sp.dma_start(xs[:, 1], x_tiles[1]).then_inc(x_landed[1], 16)
                    sp.wait_ge(comb_t_ready, 1)
                    sp.dma_start(comb_row[0:P:P // QUADS, :, :], comb_t[:, :]).then_inc(comb_row_landed, 16)

            def step(q, par, last):
                if not last:
                    sp.wait_ge(comb_t_ready, count(q, par, 1, 2))
                    sp.sem_inc(sp_passed, 1)
                    sp.wait_ge(comb_bc_ready, count(q, par, E, E))
                    sp.sem_inc(sp_passed, 1)
                    sp.dma_start(comb_row[0:P:P // QUADS, :, :], comb_t[:, :]).then_inc(comb_row_landed, 16)
                sp.wait_ge(acc_free, count(q, par, HALVES, 2 * HALVES))
                sp.sem_inc(sp_passed, 1)
                sp.dma_start(out_tiles[q * PER_SEQ + par], y[:, par]).then_inc(y_free[par], 16)

            def load(q, par):
                sp.dma_start(xs[:, par], x_tiles[(q + 1) * PER_SEQ + par]).then_inc(x_landed[par], 16)

            with sp.Fori(0, SEQS - 1) as q:
                for par in range(PER_SEQ):
                    step(q, par, False)
                    load(q, par)
            for par in range(PER_SEQ):
                step(SEQS - 1, par, par == PER_SEQ - 1)
            for par in range(PER_SEQ):
                sp.wait_ge(y_free[par], 16 * (SEQS + 1))

        @block.gpsimd
        def _(pool):
            pool.memset(ident[:], 0.0).then_inc(ident_ready, 1)
            pool.memset(minus_half[:], -0.5).then_inc(half_ready, 1)
            pool.wait_ge(ident_ready, 1)
            pool.affine_select(out=ident[:], in_=ident[:], compare_op=ALU.not_equal, fill=1.0, base=0,
                               pattern=[[-1, P]], channel_multiplier=1).then_inc(ident_ready, 1)
            pool.wait_ge(half_ready, 1)

            def root_seed(q, par):
                pool.wait_ge(var_ready, count(q, par, 1, 1))
                pool.tensor_tensor(seed[:], var_eps[:], minus_half[:], ALU.pow).then_inc(seed_ready, 1)

            def residual(q, par):
                pool.wait_ge(xn_ready, count(q, par, SUB, SUB))
                pool.tensor_tensor(xs[:, par], xs[:, par], bo_bc[:, :, :].to_broadcast([P, SUB, D]),
                                   ALU.add).then_inc(resid_ready, 1)

            def step(q, par, last):
                pool.wait_ge(comb_row_landed, count(q, par, 16, 16))
                for e in range(E):
                    pool.wait_ge(comb_bc_free, count(q, par, E, e + 1))
                    if e:
                        pool.wait_ge(comb_bc_ready, count(q, par, E, e))
                    pool.sem_inc(pool_passed, 1)
                    row = e // (E // QUADS) * (P // QUADS)
                    pool.partition_broadcast(comb_bc[:, e % RING], comb_row[row:row + 1, e % (E // QUADS), :], P).then_inc(comb_bc_ready, 1)
                    if not last and e in (SLOT_MOMENTS + RING - 1, SLOT_NORM + RING):
                        nq, npar = q + (par == 1), 1 - par
                        pool.wait_ge(comb_bc_ready, count(q, par, E, e + 1))
                        if e == SLOT_NORM + RING:
                            residual(nq, npar)
                            pool.wait_ge(resid_ready, count(nq, npar, 1, 1))
                        else:
                            root_seed(nq, npar)
                            pool.wait_ge(seed_ready, count(nq, npar, 1, 1))

            root_seed(0, 0)
            pool.wait_ge(small_landed, 48)
            residual(0, 0)
            tiles(pool, step)

        @block.scalar
        def _(act_e):
            act_e.dma_start(bias[:], attn_b).then_inc(small_landed, 16)
            act_e.dma_start(bo_bc[:, 0, :], bo.to_broadcast([P, D])).then_inc(small_landed, 16)
            act_e.dma_start(gate_b_bc[:, 0, :], gate_b.to_broadcast([P, E])).then_inc(small_landed, 16)

            def split_x(q, par, buf):
                for c in range(KC):
                    act_e.wait_ge(turned, count(q, par, KC, c + 1))
                    act_e.activation(x_hi[:, buf, c], misc[:, c], ACT.Copy).then_inc(x_hi_ready, 1)

            def split_expert(e):
                act_e.wait_ge(stage_landed[e % STAGES], 16 * (e // STAGES + 1))
                act_e.activation(exp_hi[:, e], stage[:, e % STAGES], ACT.Copy, scale=WSCALE).then_inc(exp_hi_ready, 1)

            def squash(q, par):
                act_e.wait_ge(logits_taken, count(q, par, 1, 1))
                act_e.activation(half_tanh[:], logits[:], ACT.Tanh, scale=0.5 * UNSCALE).then_inc(squashed, 1)

            def comb_out(q, par):
                act_e.wait_ge(comb_turned, count(q, par, 1, 1))
                if not is_first(q, par):
                    act_e.wait_ge(comb_row_landed, count(q, par, 16, 0))
                act_e.activation(comb_t[:, :], misc[0:E, 1], ACT.Copy).then_inc(comb_t_ready, 1)

            def step(q, par, last):
                for i, (dst, fn, scale, b) in enumerate(
                        [(tanh_w, ACT.Tanh, 0.5 * UNSCALE, half_bw)] * KC + [(tanh_k, ACT.Tanh, UNSCALE, bias[:, 1])] * KC
                        + [(u, ACT.Identity, UNSCALE, bias[:, 2])] * KC):
                    c = i % KC
                    act_e.wait_ge(proj_full, count(q, par, 3 * KC, i + 1))
                    act_e.activation(dst[:, c], misc[:, c], fn, scale=scale, bias=b[:, c:c + 1]).then_inc(proj_taken, 1)
                first = is_first(q, par)
                if first:
                    comb_out(0, 0)
                    for e in range(*AHEAD):
                        split_expert(e)
                for e in range(NE):
                    n = ep(par, e)
                    act_e.wait_ge(up_full, count(q, par, NE, e + 1))
                    act_e.activation(silu[:, n], gate_up[:, n, 0], ACT.Silu, scale=UNSCALE).then_inc(silu_ready, 1)
                    if e < E:
                        act_e.wait_ge(comb_bc_free, count(q, par, E, RING + e + 1))
                    else:
                        act_e.wait_ge(up_free, count(q, par, NE, e + 3))
                    act_e.wait_ge(h_free, count(q, par, NE, e + 1))
                    act_e.activation(h_hi[:, n], act_c[:, n], ACT.Copy).then_inc(h_hi_ready, 1)
                    if first and e + AHEAD[1] < NE:
                        split_expert(e + AHEAD[1])
                    if not last:
                        nq, npar = q + (par == 1), 1 - par
                        if e == SLOT_TURN:
                            split_x(nq, npar, npar)
                        if e == SLOT_TANH - 1:
                            squash(nq, npar)
                        if e == SLOT_COMB:
                            comb_out(nq, npar)

            act_e.wait_ge(attn_landed, 16)
            act_e.activation(router_w[:, :, 0], attn_f[:, :, RT:RT + E], ACT.Copy, scale=WSCALE).then_inc(attn_hi_ready, 1)
            split_x(0, 0, 0)
            for cols in (slice(0, WO), slice(WO, RT)):
                act_e.activation(attn_hi[:, :, cols], attn_f[:, :, cols], ACT.Copy, scale=WSCALE).then_inc(attn_hi_ready, 1)
            squash(0, 0)
            for e in range(AHEAD[0]):
                split_expert(e)
            act_e.wait_ge(const_ready, 1)
            tiles(act_e, step)

        @block.vector
        def _(dve):
            def norm_stats(q, par):
                dve.wait_ge(x_landed[par], q * 16 + 16)
                for s in range(SUB):
                    dve.bn_stats(stats[:, s], xs[:, par, s]).then_inc(stats_done, 1)

            def norm_rstd(q, par):
                for s in range(SUB):
                    dve.wait_ge(stats_done, count(q, par, SUB, s + 1))
                    dve.sem_inc(dve_passed, 1)
                    dve.bn_aggr(mv[:, s], stats[:, s]).then_inc(moments_done, 1)
                dve.wait_ge(moments_done, count(q, par, SUB, SUB))
                dve.tensor_scalar(var_eps[:], mv[:, :, 1], EPS, None, ALU.add).then_inc(var_ready, 1)

            def norm(q, par):
                dve.wait_ge(seed_ready, count(q, par, 1, 1))
                dve.tensor_tensor(n1[:], seed[:], seed[:], ALU.mult).then_inc(newton, 1)
                dve.wait_ge(newton, count(q, par, 4, 1))
                dve.tensor_tensor(n2[:], n1[:], var_eps[:], ALU.mult).then_inc(newton, 1)
                dve.wait_ge(newton, count(q, par, 4, 2))
                dve.tensor_scalar(n1[:], n2[:], -0.5, 1.5, ALU.mult, ALU.add).then_inc(newton, 1)
                dve.wait_ge(newton, count(q, par, 4, 3))
                dve.tensor_tensor(rstd[:], n1[:], seed[:], ALU.mult).then_inc(newton, 1)
                dve.wait_ge(newton, count(q, par, 4, 4))
                for s in range(SUB):
                    dve.tensor_scalar(xn[:, s], xs[:, par, s], mv[:, s, 0:1], rstd[:, s:s + 1],
                                      ALU.subtract, ALU.mult).then_inc(xn_ready, 1)

            def split_expert(e):
                dve.wait_ge(exp_hi_ready, e + 1)
                dve.scalar_tensor_tensor(out=exp_lo[:, e], in0=stage[:, e % STAGES], scalar=WSCALE, in1=exp_hi[:, e],
                                         op0=ALU.mult, op1=ALU.subtract).then_inc(exp_lo_ready, 1)

            def split_x(q, par, buf):
                for c in range(KC):
                    dve.wait_ge(x_hi_ready, count(q, par, KC, c + 1))
                    dve.tensor_tensor(x_lo[:, buf, c], misc[:, c], x_hi[:, buf, c], ALU.subtract).then_inc(x_lo_ready, 1)

            def take_logits(q, par):
                dve.wait_ge(logits_full, count(q, par, 1, 1))
                dve.tensor_reduce(logits[:], misc[:, 0, 0:SUB * 2 * E].rearrange("p (s h e) -> p s e h", h=2, e=E),
                                  AX_X, ALU.add).then_inc(logits_taken, 1)

            def mask(q, par):
                k = 0

                def done(ins):
                    nonlocal k
                    k += 1
                    ins.then_inc(route, 1)

                def ready():
                    dve.wait_ge(route, count(q, par, ROUTE_STEPS, k))

                dve.wait_ge(squashed, count(q, par, 1, 1))
                done(dve.tensor_scalar(score[:], half_tanh[:], 0.5, 0.5, ALU.mult, ALU.add))
                ready()
                done(dve.tensor_tensor(biased[:, :, 0:E], score[:], gate_b_bc[:, :, :].to_broadcast([P, SUB, E]), ALU.add))
                ready()
                dve.sem_inc(dve_passed, 1)
                for s in range(SUB):
                    done(dve.max(top8[:, s], biased[:, s]))
                ready()
                done(dve.memset(top8[:, :, TOPK:8], ABSENT))
                ready()
                dve.sem_inc(dve_passed, 1)
                for s in range(SUB):
                    done(dve.match_replace(cut[:, s], top8[:, s], biased[:, s], -2.0e38))
                ready()
                return k

            def weigh(q, par, k):
                def done(ins):
                    nonlocal k
                    k += 1
                    ins.then_inc(route, 1)
                    dve.wait_ge(route, count(q, par, ROUTE_STEPS, k))

                done(dve.tensor_tensor(chosen[:], cut[:, :, 0:E], biased[:, :, 0:E], ALU.not_equal))
                done(dve.tensor_tensor(picked[:], chosen[:], score[:], ALU.mult))
                done(dve.tensor_reduce(total[:], picked[:], AX_X, ALU.add))
                done(dve.reciprocal(inv_total[:], total[:]))
                done(dve.scalar_tensor_tensor(
                    out=comb[:], in0=picked[:], scalar=ROUTE_SCALE,
                    in1=inv_total[:, :].unsqueeze(2).to_broadcast([P, SUB, E]), op0=ALU.mult, op1=ALU.mult))
                assert k == ROUTE_STEPS

            def scan_part(q, par, part):
                c, part = divmod(part, 3)
                k = c * SCAN_STEPS

                def ready(i):
                    dve.wait_ge(scan_step, count(q, par, KC * SCAN_STEPS, k + i))

                if part == 0:
                    dve.wait_ge(proj_taken, count(q, par, 3 * KC, 3 * KC))
                    dve.tensor_scalar(gate[:], tanh_w[:, c], 0.5, 0.5, ALU.mult, ALU.add).then_inc(scan_step, 1)
                    ready(1)
                    dve.scalar_tensor_tensor(out=decay_1[:], in0=tanh_k[:, c], scalar=-1.0, in1=gate[:],
                                             op0=ALU.add, op1=ALU.mult).then_inc(scan_step, 1)
                    ready(2)
                    dve.tensor_scalar(decay[:], decay_1[:], 1.0, None, ALU.add).then_inc(scan_step, 1)
                elif part == 1:
                    dve.tensor_tensor(drive[:], gate[:], u[:, c], ALU.mult).then_inc(scan_step, 1)
                    ready(4)
                    first = 0.0 if par == 0 else state[:, c, 0, TILE - 1:TILE]
                    dve.tensor_tensor_scan(state[:, c, par], decay[:], drive[:], first,
                                           ALU.mult, ALU.add).then_inc(scan_step, 1)
                else:
                    ready(5)
                    dve.tensor_copy(s_hi[:, c], state[:, c, par]).then_inc(scan_step, 1)
                    ready(6)
                    dve.tensor_tensor(s_lo[:, c], state[:, c, par], s_hi[:, c], ALU.subtract).then_inc(scan_step, 1)

            def step(q, par, last):
                nq, npar = q + (par == 1), 1 - par
                steps = 0
                first = is_first(q, par)
                if first:
                    for e in range(*AHEAD):
                        split_expert(e)
                for e in range(NE):
                    n = ep(par, e)
                    dve.wait_ge(silu_ready, count(q, par, NE, e + 1))
                    dst = act if e < E else act_c
                    dve.scalar_tensor_tensor(out=dst[:, n], in0=gate_up[:, n, 1], scalar=UNSCALE, in1=silu[:, n],
                                             op0=ALU.mult, op1=ALU.mult).then_inc(up_free, 1)
                    if e < E:
                        dve.wait_ge(comb_bc_ready, count(q, par, E, e + 1))
                        dve.wait_ge(up_free, count(q, par, NE, e + 3))
                        dve.tensor_tensor(act_c[:, n], act[:, n], comb_bc[:, e % RING], ALU.mult).then_inc(comb_bc_free, 1)
                    dve.wait_ge(h_hi_ready, count(q, par, NE, e + 1))
                    dve.tensor_tensor(h_lo[:, n], act_c[:, n], h_hi[:, n], ALU.subtract).then_inc(h_lo_ready, 1)
                    if first and e + AHEAD[1] < NE:
                        split_expert(e + AHEAD[1])
                    if e in SLOT_SCAN:
                        scan_part(q, par, SLOT_SCAN.index(e))
                    if last:
                        continue
                    if e == SLOT_STATS:
                        norm_stats(nq, npar)
                    if e == SLOT_MOMENTS:
                        norm_rstd(nq, npar)
                    if e == SLOT_NORM:
                        norm(nq, npar)
                    if e == SLOT_TURN:
                        split_x(nq, npar, npar)
                    if e == SLOT_ROUTE:
                        take_logits(nq, npar)
                    if e == SLOT_TANH:
                        steps = mask(nq, npar)
                    if e == SLOT_WEIGH:
                        weigh(nq, npar, steps)
                dve.wait_ge(h_free, count(q, par, NE, NE + 2))
                dve.wait_ge(resid_ready, count(q, par, 1, 1))
                dve.wait_ge(y_free[par], q * 16 + 16)
                w = SUB // HALVES
                for b in range(HALVES):
                    dve.scalar_tensor_tensor(out=y[:, par, b * w:(b + 1) * w], in0=acc[:, b * w:(b + 1) * w], scalar=UNSCALE,
                                             in1=xs[:, par, b * w:(b + 1) * w], op0=ALU.mult, op1=ALU.add).then_inc(acc_free, 1)

            dve.memset(biased[:, :, E:E + PADS], ABSENT).then_inc(up_free, 2)
            dve.memset(credit[:, 0:1], 0.0).then_inc(acc_free, HALVES)
            dve.memset(credit[:, 1:2], 0.0).then_inc(h_free, 2)
            dve.memset(credit[:, 2:3], 0.0).then_inc(comb_bc_free, RING)
            for i in range(2):
                dve.memset(credit[:, 3 + i:4 + i], 0.0).then_inc(y_free[i], 16)
            norm_stats(0, 0)
            norm_rstd(0, 0)
            norm(0, 0)
            dve.wait_ge(small_landed, 48)
            dve.tensor_scalar(half_bw[:], bias[:, 0], 0.5, None, ALU.mult).then_inc(const_ready, 1)
            dve.wait_ge(attn_hi_ready, 1)
            dve.scalar_tensor_tensor(out=router_w[:, :, 1], in0=attn_f[:, :, RT:RT + E], scalar=WSCALE, in1=router_w[:, :, 0],
                                     op0=ALU.mult, op1=ALU.subtract).then_inc(attn_lo_ready, 1)
            split_x(0, 0, 0)
            for i, cols in enumerate((slice(0, WO), slice(WO, RT))):
                dve.wait_ge(attn_hi_ready, 2 + i)
                dve.scalar_tensor_tensor(out=attn_lo[:, :, cols], in0=attn_f[:, :, cols], scalar=WSCALE,
                                         in1=attn_hi[:, :, cols], op0=ALU.mult, op1=ALU.subtract).then_inc(attn_lo_ready, 1)
            dve.wait_ge(up_free, 2)
            take_logits(0, 0)
            weigh(0, 0, mask(0, 0))
            for e in range(AHEAD[0]):
                split_expert(e)
            tiles(dve, step)

        @block.tensor
        def _(pe):
            def turn(q, par):
                for c in range(KC):
                    for s in range(SUB):
                        pe.wait_ge(xn_ready, count(q, par, SUB, s + 1))
                        last = pe.transpose(misc[:, c, s * P:(s + 1) * P], xn[:, s, c * P:(c + 1) * P], ident[:])
                    last.then_inc(turned, 1)

            def router(q, par, buf):
                pe.wait_ge(x_lo_ready, count(q, par, KC, KC))
                for s in range(SUB):
                    terms = [(xp, c) for c in range(KC) for xp in (x_hi, x_lo)]
                    for i, (xp, c) in enumerate(terms):
                        last = pe.matmul(misc[:, 0, s * 2 * E:(s + 1) * 2 * E], xp[:, buf, c, s * P:(s + 1) * P],
                                         router_w[:, c, :, :].rearrange("p h e -> p (h e)"),
                                         start=(i == 0), stop=(i == len(terms) - 1))
                last.then_inc(logits_full, 1)

            def turn_comb(q, par):
                pe.wait_ge(route, count(q, par, ROUTE_STEPS, ROUTE_STEPS))
                for s in range(SUB):
                    last = pe.transpose(misc[0:E, 1, s * P:(s + 1) * P], comb[:, s], ident[:])
                last.then_inc(comb_turned, 1)

            def product(dst, w_hi, w_lo, x_h, x_l):
                for c in range(KC):
                    pe.matmul(dst, w_hi(c), x_h(c), start=(c == 0), stop=False)
                    pe.matmul(dst, w_hi(c), x_l(c), start=False, stop=False)
                    last = pe.matmul(dst, w_lo(c), x_h(c), start=False, stop=(c == KC - 1))
                return last

            def project(q, par):
                for i in range(3 * KC):
                    if i == 0:
                        pe.wait_ge(logits_taken, count(q, par, 1, 1))
                    elif i == 1 and not is_first(q, par):
                        pe.wait_ge(comb_t_ready, count(q, par, 1, 1))
                    elif i > 1:
                        pe.wait_ge(proj_taken, count(q, par, 3 * KC, i - 1))
                    product(misc[:, i % 2], lambda c: attn_hi[:, c, i * P:(i + 1) * P], lambda c: attn_lo[:, c, i * P:(i + 1) * P],
                            lambda c: x_hi[:, par, c], lambda c: x_lo[:, par, c]).then_inc(proj_full, 1)

            def up(q, par, e):
                n = ep(par, e)
                pe.wait_ge(up_free, count(q, par, NE, e + 1))
                for g in range(2):
                    last = product(gate_up[:, n, g],
                                   lambda c: exp_hi[:, e, c * 2 * I + g * I:c * 2 * I + (g + 1) * I],
                                   lambda c: exp_lo[:, e, c * 2 * I + g * I:c * 2 * I + (g + 1) * I],
                                   lambda c: x_hi[:, par, c], lambda c: x_lo[:, par, c])
                last.then_inc(up_full, 1)

            def add_to_acc(v_hi, v_lo, w_hi, w_lo, first=False, end=False):
                for s in range(SUB):
                    cols = slice(s * P, (s + 1) * P)
                    for i, (v, w) in enumerate(((v_hi, w_hi), (v_hi, w_lo), (v_lo, w_hi))):
                        last = pe.matmul(acc[:, s], v[:, cols], w, start=(first and i == 0 and s % 2 == 0),
                                         stop=(end and i == 2), skip_group_check=True)
                return last

            def down(q, par, e, end=False):
                n = ep(par, e)
                if e == 0:
                    pe.wait_ge(acc_free, count(q, par, HALVES, HALVES))
                pe.wait_ge(h_hi_ready, count(q, par, NE, e + 1))
                pe.wait_ge(h_lo_ready, count(q, par, NE, e + 1))
                last = add_to_acc(h_hi[:, n], h_lo[:, n], exp_hi[:, e, DOWN:DOWN + D], exp_lo[:, e, DOWN:DOWN + D],
                                  first=(e == 0), end=end)
                last.then_inc(h_free, 1)

            def recurrence_out(q, par):
                pe.wait_ge(scan_step, count(q, par, KC * SCAN_STEPS, KC * SCAN_STEPS))
                for c in range(KC):
                    add_to_acc(s_hi[:, c], s_lo[:, c], attn_hi[:, c, WO:WO + D], attn_lo[:, c, WO:WO + D])

            def step(q, par, last):
                nq, npar = q + (par == 1), 1 - par
                project(q, par)
                first = is_first(q, par)
                if first:
                    pe.wait_ge(proj_taken, 3 * KC)
                    turn_comb(0, 0)
                for e in range(NE):
                    if first:
                        pe.wait_ge(exp_lo_ready, e + 1)
                    up(q, par, e)
                    if e >= LAG:
                        down(q, par, e - LAG)
                    if last:
                        continue
                    if e == SLOT_TURN:
                        pe.wait_ge(proj_taken, count(q, par, 3 * KC, 3 * KC))
                        turn(nq, npar)
                    if e == SLOT_ROUTE:
                        router(nq, npar, npar)
                    if e == SLOT_COMB:
                        turn_comb(nq, npar)
                recurrence_out(q, par)
                down(q, par, NE - 2)
                down(q, par, NE - 1, end=True)

            pe.wait_ge(ident_ready, 2)
            turn(0, 0)
            pe.wait_ge(attn_lo_ready, 1)
            router(0, 0, 0)
            pe.wait_ge(attn_lo_ready, 3)
            tiles(pe, step)


_OUTS = [((8, 1024, 256), 'float32')]


def kernel(L0_attn_x, L0_attn_Wp, L0_attn_bp, L0_attn_Wu, L0_attn_bu, L0_attn_Wo, L0_attn_bo, L0_ffn_input_ids,
           L0_ffn_gate_w, L0_ffn_gate_b, L0_ffn_w13, L0_ffn_w2, L0_ffn_w13_s, L0_ffn_w2_s):
    import numpy as np
    import concourse.bacc as bacc
    from concourse.bass_utils import run_bass_kernel_spmd

    def chunks(w):
        w = np.asarray(w)
        return w.reshape(w.shape[0] // P, P, w.shape[1]).transpose(1, 0, 2)

    x = np.asarray(L0_attn_x)
    d = x.shape[-1]
    attn_w = np.concatenate([chunks(np.asarray(L0_attn_Wp)[:, :2 * d]), chunks(L0_attn_Wu), chunks(L0_attn_Wo),
                             chunks(np.asarray(L0_ffn_gate_w).T)], axis=2)
    attn_b = np.concatenate([np.asarray(L0_attn_bp)[:2 * d], np.asarray(L0_attn_bu)]).reshape(3, d // P, P).transpose(2, 0, 1)
    w13 = np.concatenate([np.asarray(L0_ffn_w13), np.asarray(L0_ffn_w13_s)[None]])
    w2 = np.concatenate([np.asarray(L0_ffn_w2), np.asarray(L0_ffn_w2_s)[None]])
    ne, two_i, _ = w13.shape
    up = w13.transpose(0, 2, 1).reshape(ne, d // P, P, two_i).transpose(0, 2, 1, 3).reshape(ne, P, -1)
    expert_w = np.concatenate([up, w2.transpose(0, 2, 1)], axis=2)
    arrays = {
        "x": x.reshape(-1, d), "attn_w": attn_w, "attn_b": attn_b, "bo": np.asarray(L0_attn_bo)[None],
        "gate_b": np.asarray(L0_ffn_gate_b)[None], "expert_w": expert_w,
    }
    nc = bacc.Bacc("TRN2", target_bir_lowering=False, num_devices=1)
    args = []
    for name in arrays:
        arrays[name] = np.ascontiguousarray(arrays[name])
        args.append(nc.dram_tensor(name, arrays[name].shape, mybir.dt.from_np(arrays[name].dtype), kind="ExternalInput").ap())
    out = nc.dram_tensor("out", arrays["x"].shape, F32, kind="ExternalOutput").ap()
    scan_moe_kernel(nc, *args, out)
    r = run_bass_kernel_spmd(nc, [arrays], core_ids=[0])
    return r.results[0]["out"].reshape(x.shape)
```

```python
from contextlib import ExitStack

import concourse.bass as bass
from concourse import mybir

F32 = mybir.dt.float32
F16 = mybir.dt.float16
ALU = mybir.AluOpType
ACT = mybir.ActivationFunctionType
AX_X = mybir.AxisListType.X

P = 128
TILE = 512
SUB = TILE // P
TOPK = 4
ROUTE_SCALE = 2.5
EPS = 1e-5
WSCALE = 64.0
UNSCALE = 1.0 / WSCALE
ABSENT = -3.0e38
PADS = 4
BLOCK = 32
QUADS = 4
STAGES = 12
AHEAD = (3, 7, 15)
FIRST_LOADS = 4
RING = 4
LAG = 2

SLOT_STATS, SLOT_MOMENTS, SLOT_NORM, SLOT_SPLIT, SLOT_ROUTE, SLOT_TANH, SLOT_WEIGH = 2, 3, 4, 5, 9, 10, 12
SLOT_SCAN = (6, 7, 8, 11, 13, 14)


def scan_moe_kernel(nc, x, attn_w, attn_b, bo, gate_b, expert_w, out):
    tokens, D = x.shape
    KC = D // P
    E = gate_b.shape[1]
    NE = E + 1
    I = (expert_w.shape[2] - D) // (2 * KC)
    TILES = tokens // TILE
    PER_SEQ = 2
    SEQS = TILES // PER_SEQ
    assert I == P and KC == 2 and TILES % PER_SEQ == 0

    x_tiles = x.rearrange("(t s p) d -> t p s d", s=SUB, p=P)
    out_tiles = out.rearrange("(t s p) d -> t p s d", s=SUB, p=P)

    with ExitStack() as ctx:
        def sb(name, shape, dt=F32):
            return ctx.enter_context(nc.sbuf_tensor(name, shape, dt))

        def sem(name):
            return ctx.enter_context(nc.semaphore(name))

        AW = 3 * D + D + E
        attn_f = sb("attn_f", [P, KC, AW])
        attn_hi = sb("attn_hi", [P, KC, 4 * D], F16)
        attn_lo = sb("attn_lo", [P, KC, 4 * D], F16)
        WO, RT = 3 * D, 4 * D
        EW = 2 * I * KC + D
        stage = sb("stage", [P, STAGES, EW])
        exp_hi = sb("exp_hi", [P, NE, EW], F16)
        exp_lo = sb("exp_lo", [P, NE, EW], F16)
        DOWN = 2 * I * KC
        bias = sb("bias", [P, 3, KC])
        half_bw = sb("half_bw", [P, KC])
        bo_bc = sb("bo_bc", [P, 1, D])
        gate_b_bc = sb("gate_b_bc", [P, 1, E])
        credit = sb("credit", [P, 5])
        first_silu = sb("first_silu", [P, SUB])
        minus_half = sb("minus_half", [P, SUB])

        xs = sb("xs", [P, 2, SUB, D])
        xn = sb("xn", [P, SUB, D])
        xn_parts = sb("xn_parts", [P, SUB, 2, D], F16)
        x_t = sb("x_t", [P, 2, SUB, 2, KC, P], F16)
        stats = sb("stats", [P, SUB, 6])
        mv = sb("mv", [P, SUB, 2])
        var_eps = sb("var_eps", [P, SUB])
        seed = sb("seed", [P, SUB])
        n1 = sb("n1", [P, SUB])
        n2 = sb("n2", [P, SUB])
        rstd = sb("rstd", [P, SUB])
        router_w = sb("router_w", [P, KC, 2, E], F16)
        logits = sb("logits", [P, SUB, E])
        half_tanh = sb("half_tanh", [P, SUB, E])
        score = sb("score", [P, SUB, E])
        biased = sb("biased", [P, SUB, E + PADS])
        top8 = sb("top8", [P, SUB, 8])
        cut = sb("cut", [P, SUB, E + PADS])
        chosen = sb("chosen", [P, SUB, E])
        picked = sb("picked", [P, SUB, E])
        total = sb("total", [P, SUB])
        inv_total = sb("inv_total", [P, SUB])
        comb = sb("comb", [P, SUB, BLOCK])
        comb_t = sb("comb_t", [P, SUB, BLOCK])
        comb_row = sb("comb_row", [P, E // QUADS, TILE])
        comb_bc = sb("comb_bc", [P, RING, TILE])
        tanh_w = sb("tanh_w", [P, KC, TILE])
        tanh_k = sb("tanh_k", [P, KC, TILE])
        u = sb("u", [P, KC, TILE])
        gate = sb("gate", [P, TILE])
        decay_1 = sb("decay_1", [P, TILE])
        decay = sb("decay", [P, TILE])
        drive = sb("drive", [P, TILE])
        state = sb("state", [P, KC, 2, TILE])
        s_hi = sb("s_hi", [P, KC, TILE], F16)
        s_lo = sb("s_lo", [P, KC, TILE], F16)
        silu = sb("silu", [P, 2, TILE])
        act = sb("act", [P, 2, TILE])
        act_c = sb("act_c", [P, 2, TILE])
        h_hi = sb("h_hi", [P, 2, TILE], F16)
        h_lo = sb("h_lo", [P, 2, TILE], F16)
        y = sb("y", [P, 2, SUB, D])

        acc = ctx.enter_context(nc.psum_tensor("acc", [P, SUB, D], F32))
        gate_up = ctx.enter_context(nc.psum_tensor("gate_up", [P, 2, 2, TILE], F32))
        misc = ctx.enter_context(nc.psum_tensor("misc", [P, 2, TILE], F32))

        attn_landed = sem("attn_landed")
        small_landed = sem("small_landed")
        stage_landed = [sem(f"stage_landed{i}") for i in range(STAGES)]
        x_landed = [sem(f"x_landed{i}") for i in range(2)]
        half_ready = sem("half_ready")
        const_ready = sem("const_ready")
        comb_zeroed = sem("comb_zeroed")
        attn_hi_ready = sem("attn_hi_ready")
        attn_lo_ready = sem("attn_lo_ready")
        exp_hi_ready = sem("exp_hi_ready")
        exp_lo_ready = sem("exp_lo_ready")
        stats_done = sem("stats_done")
        moments_done = sem("moments_done")
        var_ready = sem("var_ready")
        seed_ready = sem("seed_ready")
        newton = sem("newton")
        xn_ready = sem("xn_ready")
        resid_ready = sem("resid_ready")
        xn_hi_ready = sem("xn_hi_ready")
        xn_lo_ready = sem("xn_lo_ready")
        turned = sem("turned")
        logits_full = sem("logits_full")
        logits_taken = sem("logits_taken")
        squashed = sem("squashed")
        route = sem("route")
        comb_row_landed = sem("comb_row_landed")
        comb_bc_ready = sem("comb_bc_ready")
        comb_bc_free = sem("comb_bc_free")
        proj_full = sem("proj_full")
        proj_taken = sem("proj_taken")
        scan_step = sem("scan_step")
        up_full = sem("up_full")
        silu_ready = sem("silu_ready")
        up_free = sem("up_free")
        h_hi_ready = sem("h_hi_ready")
        h_lo_ready = sem("h_lo_ready")
        h_free = sem("h_free")
        acc_free = sem("acc_free")
        y_free = [sem(f"y_free{i}") for i in range(2)]

        dve_passed = sem("dve_passed")
        pool_passed = sem("pool_passed")
        sp_passed = sem("sp_passed")

        ROUTE_STEPS = 2 + SUB + 1 + SUB + 6
        SCAN_STEPS = 7
        HALVES = 2
        TURN = 16
        ROW = 16 * QUADS

        block = ctx.enter_context(nc.Block())

        def tiles(eng, body):
            for par in range(PER_SEQ):
                body(0, par, False)
            with eng.Fori(1, SEQS - 1) as q:
                for par in range(PER_SEQ):
                    body(q, par, False)
            for par in range(PER_SEQ):
                body(SEQS - 1, par, par == PER_SEQ - 1)

        def count(q, par, per_tile, k):
            return q * (PER_SEQ * per_tile) + (par * per_tile + k)

        def is_first(q, par):
            return isinstance(q, int) and q == 0 and par == 0

        def ep(par, e):
            return (par * NE + e) % 2

        @block.sync
        def _(sp):
            def turn_x(par):
                sp.dma_start_transpose(x_t[:, par].rearrange("p s h c n -> p (s h c) n"),
                                       xn_parts[:].rearrange("p s h d -> p (s h d)")).then_inc(turned, 16)

            def comb_rows():
                for k in range(QUADS):
                    src = comb_t[k * BLOCK:k * BLOCK + E, :, :]
                    dst = comb_row[0:P:P // QUADS, :, :].rearrange("a b (s k n) -> a b s k n", s=SUB, n=BLOCK)
                    sp.dma_start(dst[:, :, :, k, :], src).then_inc(comb_row_landed, 16)

            def load_expert(e):
                if e >= STAGES:
                    sp.wait_ge(exp_lo_ready, e - STAGES + 1)
                sp.dma_start(stage[:, e % STAGES], expert_w[e]).then_inc(stage_landed[e % STAGES], 16)

            sp.dma_start(xs[:, 0], x_tiles[0]).then_inc(x_landed[0], 16)
            sp.dma_start(attn_f[:], attn_w).then_inc(attn_landed, 16)
            for e in range(FIRST_LOADS):
                load_expert(e)
            sp.wait_ge(xn_hi_ready, 1)
            sp.wait_ge(xn_lo_ready, 1)
            turn_x(0)
            for e in range(FIRST_LOADS, NE):
                load_expert(e)
                if e == STAGES - 1:
                    sp.dma_start(xs[:, 1], x_tiles[1]).then_inc(x_landed[1], 16)
                    sp.wait_ge(route, ROUTE_STEPS)
                    comb_rows()

            def step(q, par, last):
                if not last:
                    nq, npar = q + (par == 1), 1 - par
                    sp.wait_ge(xn_lo_ready, count(nq, npar, 1, 1))
                    sp.sem_inc(sp_passed, 1)
                    turn_x(npar)
                    sp.wait_ge(route, count(nq, npar, ROUTE_STEPS, ROUTE_STEPS))
                    sp.sem_inc(sp_passed, 1)
                    sp.wait_ge(comb_bc_ready, count(q, par, E, E))
                    sp.sem_inc(sp_passed, 1)
                    comb_rows()
                sp.wait_ge(acc_free, count(q, par, HALVES, 2 * HALVES))
                sp.sem_inc(sp_passed, 1)
                sp.dma_start(out_tiles[q * PER_SEQ + par], y[:, par]).then_inc(y_free[par], 16)

            def load(q, par):
                sp.dma_start(xs[:, par], x_tiles[(q + 1) * PER_SEQ + par]).then_inc(x_landed[par], 16)

            for par in range(PER_SEQ):
                step(0, par, False)
                load(0, par)
            with sp.Fori(1, SEQS - 1) as q:
                for par in range(PER_SEQ):
                    step(q, par, False)
                    load(q, par)
            for par in range(PER_SEQ):
                step(SEQS - 1, par, par == PER_SEQ - 1)
            for par in range(PER_SEQ):
                sp.wait_ge(y_free[par], 16 * (SEQS + 1))

        @block.gpsimd
        def _(pool):
            pool.memset(minus_half[:], -0.5).then_inc(half_ready, 1)
            pool.wait_ge(half_ready, 1)

            def root_seed(q, par):
                pool.wait_ge(var_ready, count(q, par, 1, 1))
                pool.tensor_tensor(seed[:], var_eps[:], minus_half[:], ALU.pow).then_inc(seed_ready, 1)

            def residual(q, par):
                pool.wait_ge(xn_ready, count(q, par, SUB, SUB))
                pool.tensor_tensor(xs[:, par], xs[:, par], bo_bc[:, :, :].to_broadcast([P, SUB, D]),
                                   ALU.add).then_inc(resid_ready, 1)

            def step(q, par, last):
                pool.wait_ge(comb_row_landed, count(q, par, ROW, ROW))
                for e in range(E):
                    pool.wait_ge(comb_bc_free, count(q, par, E, e + 1))
                    if e:
                        pool.wait_ge(comb_bc_ready, count(q, par, E, e))
                    pool.sem_inc(pool_passed, 1)
                    row = e // (E // QUADS) * (P // QUADS)
                    pool.partition_broadcast(comb_bc[:, e % RING], comb_row[row:row + 1, e % (E // QUADS), :], P).then_inc(comb_bc_ready, 1)
                    if not last and e in (SLOT_MOMENTS + RING - 1, SLOT_NORM + RING):
                        nq, npar = q + (par == 1), 1 - par
                        pool.wait_ge(comb_bc_ready, count(q, par, E, e + 1))
                        if e == SLOT_NORM + RING:
                            residual(nq, npar)
                            pool.wait_ge(resid_ready, count(nq, npar, 1, 1))
                        else:
                            root_seed(nq, npar)
                            pool.wait_ge(seed_ready, count(nq, npar, 1, 1))

            root_seed(0, 0)
            pool.wait_ge(small_landed, 48)
            residual(0, 0)
            tiles(pool, step)

        @block.scalar
        def _(act_e):
            act_e.dma_start(bias[:], attn_b).then_inc(small_landed, 16)
            act_e.dma_start(bo_bc[:, 0, :], bo.to_broadcast([P, D])).then_inc(small_landed, 16)
            act_e.dma_start(gate_b_bc[:, 0, :], gate_b.to_broadcast([P, E])).then_inc(small_landed, 16)

            def split_x(q, par):
                act_e.wait_ge(xn_ready, count(q, par, SUB, SUB))
                if not is_first(q, par):
                    act_e.wait_ge(turned, count(q, par, TURN, 0))
                act_e.activation(xn_parts[:, :, 0], xn[:], ACT.Copy).then_inc(xn_hi_ready, 1)

            def split_expert(e):
                act_e.wait_ge(stage_landed[e % STAGES], 16 * (e // STAGES + 1))
                act_e.activation(exp_hi[:, e], stage[:, e % STAGES], ACT.Copy, scale=WSCALE).then_inc(exp_hi_ready, 1)

            def squash(q, par):
                act_e.wait_ge(logits_taken, count(q, par, 1, 1))
                act_e.activation(half_tanh[:], logits[:], ACT.Tanh, scale=0.5 * UNSCALE).then_inc(squashed, 1)

            def step(q, par, last):
                for i, (dst, fn, scale, b) in enumerate(
                        [(tanh_w, ACT.Tanh, 0.5 * UNSCALE, half_bw)] * KC + [(tanh_k, ACT.Tanh, UNSCALE, bias[:, 1])] * KC
                        + [(u, ACT.Identity, UNSCALE, bias[:, 2])] * KC):
                    c = i % KC
                    act_e.wait_ge(proj_full, count(q, par, 3 * KC, i + 1))
                    act_e.activation(dst[:, c], misc[:, c], fn, scale=scale, bias=b[:, c:c + 1]).then_inc(proj_taken, 1)
                    if is_first(q, par):
                        split_expert(AHEAD[1] + i)
                first = is_first(q, par)
                if first:
                    for e in range(AHEAD[1] + 3 * KC, AHEAD[2]):
                        split_expert(e)
                for e in range(NE):
                    n = ep(par, e)
                    act_e.wait_ge(up_full, count(q, par, NE, e + 1))
                    act_e.activation(silu[:, n], gate_up[:, n, 0], ACT.Silu, scale=UNSCALE).then_inc(silu_ready, 1)
                    if e < E:
                        act_e.wait_ge(comb_bc_free, count(q, par, E, RING + e + 1))
                    else:
                        act_e.wait_ge(up_free, count(q, par, NE, e + 3))
                    act_e.wait_ge(h_free, count(q, par, NE, e + 1))
                    act_e.activation(h_hi[:, n], act_c[:, n], ACT.Copy).then_inc(h_hi_ready, 1)
                    if first and e + AHEAD[2] < NE:
                        split_expert(e + AHEAD[2])
                    if not last:
                        nq, npar = q + (par == 1), 1 - par
                        if e == SLOT_SPLIT:
                            split_x(nq, npar)
                        if e == SLOT_TANH - 1:
                            squash(nq, npar)

            act_e.wait_ge(half_ready, 1)
            act_e.activation(first_silu[:], minus_half[:], ACT.Silu)
            split_x(0, 0)
            act_e.wait_ge(attn_landed, 16)
            act_e.activation(router_w[:, :, 0], attn_f[:, :, RT:RT + E], ACT.Copy, scale=WSCALE).then_inc(attn_hi_ready, 1)
            for cols in (slice(0, WO), slice(WO, RT)):
                act_e.activation(attn_hi[:, :, cols], attn_f[:, :, cols], ACT.Copy, scale=WSCALE).then_inc(attn_hi_ready, 1)
            for e in range(AHEAD[0]):
                split_expert(e)
            squash(0, 0)
            for e in range(AHEAD[0], AHEAD[1]):
                split_expert(e)
            act_e.wait_ge(const_ready, 1)
            tiles(act_e, step)

        @block.vector
        def _(dve):
            def norm_stats(q, par):
                dve.wait_ge(x_landed[par], q * 16 + 16)
                for s in range(SUB):
                    dve.bn_stats(stats[:, s], xs[:, par, s]).then_inc(stats_done, 1)

            def norm_rstd(q, par):
                for s in range(SUB):
                    dve.wait_ge(stats_done, count(q, par, SUB, s + 1))
                    dve.sem_inc(dve_passed, 1)
                    dve.bn_aggr(mv[:, s], stats[:, s]).then_inc(moments_done, 1)
                dve.wait_ge(moments_done, count(q, par, SUB, SUB))
                dve.tensor_scalar(var_eps[:], mv[:, :, 1], EPS, None, ALU.add).then_inc(var_ready, 1)

            def norm(q, par):
                dve.wait_ge(seed_ready, count(q, par, 1, 1))
                dve.tensor_tensor(n1[:], seed[:], seed[:], ALU.mult).then_inc(newton, 1)
                dve.wait_ge(newton, count(q, par, 4, 1))
                dve.tensor_tensor(n2[:], n1[:], var_eps[:], ALU.mult).then_inc(newton, 1)
                dve.wait_ge(newton, count(q, par, 4, 2))
                dve.tensor_scalar(n1[:], n2[:], -0.5, 1.5, ALU.mult, ALU.add).then_inc(newton, 1)
                dve.wait_ge(newton, count(q, par, 4, 3))
                dve.tensor_tensor(rstd[:], n1[:], seed[:], ALU.mult).then_inc(newton, 1)
                dve.wait_ge(newton, count(q, par, 4, 4))
                for s in range(SUB):
                    dve.tensor_scalar(xn[:, s], xs[:, par, s], mv[:, s, 0:1], rstd[:, s:s + 1],
                                      ALU.subtract, ALU.mult).then_inc(xn_ready, 1)

            def split_expert(e):
                dve.wait_ge(exp_hi_ready, e + 1)
                dve.scalar_tensor_tensor(out=exp_lo[:, e], in0=stage[:, e % STAGES], scalar=WSCALE, in1=exp_hi[:, e],
                                         op0=ALU.mult, op1=ALU.subtract).then_inc(exp_lo_ready, 1)

            def split_x(q, par):
                dve.wait_ge(xn_hi_ready, count(q, par, 1, 1))
                if not is_first(q, par):
                    dve.wait_ge(turned, count(q, par, TURN, 0))
                dve.tensor_tensor(xn_parts[:, :, 1], xn[:], xn_parts[:, :, 0], ALU.subtract).then_inc(xn_lo_ready, 1)

            def take_logits(q, par):
                dve.wait_ge(logits_full, count(q, par, 1, 1))
                dve.tensor_reduce(logits[:], misc[:, 0, 0:SUB * 2 * E].rearrange("p (s h e) -> p s e h", h=2, e=E),
                                  AX_X, ALU.add).then_inc(logits_taken, 1)

            def mask(q, par):
                k = 0

                def done(ins):
                    nonlocal k
                    k += 1
                    ins.then_inc(route, 1)

                def ready():
                    dve.wait_ge(route, count(q, par, ROUTE_STEPS, k))

                dve.wait_ge(squashed, count(q, par, 1, 1))
                done(dve.tensor_scalar(score[:], half_tanh[:], 0.5, 0.5, ALU.mult, ALU.add))
                ready()
                done(dve.tensor_tensor(biased[:, :, 0:E], score[:], gate_b_bc[:, :, :].to_broadcast([P, SUB, E]), ALU.add))
                ready()
                dve.sem_inc(dve_passed, 1)
                for s in range(SUB):
                    done(dve.max(top8[:, s], biased[:, s]))
                ready()
                done(dve.memset(top8[:, :, TOPK:8], ABSENT))
                ready()
                dve.sem_inc(dve_passed, 1)
                for s in range(SUB):
                    done(dve.match_replace(cut[:, s], top8[:, s], biased[:, s], -2.0e38))
                ready()
                return k

            def weigh(q, par, k):
                def done(ins):
                    nonlocal k
                    k += 1
                    ins.then_inc(route, 1)
                    dve.wait_ge(route, count(q, par, ROUTE_STEPS, k))

                done(dve.tensor_tensor(chosen[:], cut[:, :, 0:E], biased[:, :, 0:E], ALU.not_equal))
                done(dve.tensor_tensor(picked[:], chosen[:], score[:], ALU.mult))
                done(dve.tensor_reduce(total[:], picked[:], AX_X, ALU.add))
                done(dve.reciprocal(inv_total[:], total[:]))
                done(dve.scalar_tensor_tensor(
                    out=comb[:, :, 0:E], in0=picked[:], scalar=ROUTE_SCALE,
                    in1=inv_total[:, :].unsqueeze(2).to_broadcast([P, SUB, E]), op0=ALU.mult, op1=ALU.mult))
                if not is_first(q, par):
                    dve.wait_ge(comb_row_landed, count(q, par, ROW, 0))
                done(dve.transpose(comb_t[:].rearrange("p s n -> p (s n)"), comb[:].rearrange("p s n -> p (s n)")))
                assert k == ROUTE_STEPS

            def scan_part(q, par, part):
                c, part = divmod(part, 3)
                k = c * SCAN_STEPS

                def ready(i):
                    dve.wait_ge(scan_step, count(q, par, KC * SCAN_STEPS, k + i))

                if part == 0:
                    dve.wait_ge(proj_taken, count(q, par, 3 * KC, 3 * KC))
                    dve.tensor_scalar(gate[:], tanh_w[:, c], 0.5, 0.5, ALU.mult, ALU.add).then_inc(scan_step, 1)
                    ready(1)
                    dve.scalar_tensor_tensor(out=decay_1[:], in0=tanh_k[:, c], scalar=-1.0, in1=gate[:],
                                             op0=ALU.add, op1=ALU.mult).then_inc(scan_step, 1)
                    ready(2)
                    dve.tensor_scalar(decay[:], decay_1[:], 1.0, None, ALU.add).then_inc(scan_step, 1)
                elif part == 1:
                    dve.tensor_tensor(drive[:], gate[:], u[:, c], ALU.mult).then_inc(scan_step, 1)
                    ready(4)
                    first = 0.0 if par == 0 else state[:, c, 0, TILE - 1:TILE]
                    dve.tensor_tensor_scan(state[:, c, par], decay[:], drive[:], first,
                                           ALU.mult, ALU.add).then_inc(scan_step, 1)
                else:
                    ready(5)
                    dve.tensor_copy(s_hi[:, c], state[:, c, par]).then_inc(scan_step, 1)
                    ready(6)
                    dve.tensor_tensor(s_lo[:, c], state[:, c, par], s_hi[:, c], ALU.subtract).then_inc(scan_step, 1)

            steps = 0

            def between(q, par, e, last):
                nonlocal steps
                nq, npar = q + (par == 1), 1 - par
                if is_first(q, par) and e + AHEAD[2] < NE:
                    split_expert(e + AHEAD[2])
                if e in SLOT_SCAN:
                    scan_part(q, par, SLOT_SCAN.index(e))
                if last:
                    return
                if e == SLOT_STATS:
                    norm_stats(nq, npar)
                if e == SLOT_MOMENTS:
                    norm_rstd(nq, npar)
                if e == SLOT_NORM:
                    norm(nq, npar)
                if e == SLOT_SPLIT:
                    split_x(nq, npar)
                if e == SLOT_ROUTE:
                    take_logits(nq, npar)
                if e == SLOT_TANH:
                    steps = mask(nq, npar)
                if e == SLOT_WEIGH:
                    weigh(nq, npar, steps)

            def step(q, par, last):
                first = is_first(q, par)
                if first:
                    for e in range(AHEAD[1], AHEAD[2]):
                        split_expert(e)
                for e in range(NE):
                    n = ep(par, e)
                    dve.wait_ge(silu_ready, count(q, par, NE, e + 1))
                    dst = act if e < E else act_c
                    dve.scalar_tensor_tensor(out=dst[:, n], in0=gate_up[:, n, 1], scalar=UNSCALE, in1=silu[:, n],
                                             op0=ALU.mult, op1=ALU.mult).then_inc(up_free, 1)
                    if e < E:
                        dve.wait_ge(comb_bc_ready, count(q, par, E, e + 1))
                        dve.wait_ge(up_free, count(q, par, NE, e + 3))
                        dve.tensor_tensor(act_c[:, n], act[:, n], comb_bc[:, e % RING], ALU.mult).then_inc(comb_bc_free, 1)
                    between(q, par, e, last)
                    dve.wait_ge(h_hi_ready, count(q, par, NE, e + 1))
                    dve.tensor_tensor(h_lo[:, n], act_c[:, n], h_hi[:, n], ALU.subtract).then_inc(h_lo_ready, 1)
                dve.wait_ge(h_free, count(q, par, NE, NE + 2))
                dve.wait_ge(resid_ready, count(q, par, 1, 1))
                dve.wait_ge(y_free[par], q * 16 + 16)
                w = SUB // HALVES
                for b in range(HALVES):
                    dve.scalar_tensor_tensor(out=y[:, par, b * w:(b + 1) * w], in0=acc[:, b * w:(b + 1) * w], scalar=UNSCALE,
                                             in1=xs[:, par, b * w:(b + 1) * w], op0=ALU.mult, op1=ALU.add).then_inc(acc_free, 1)

            dve.memset(biased[:, :, E:E + PADS], ABSENT).then_inc(up_free, 2)
            dve.memset(credit[:, 0:1], 0.0).then_inc(acc_free, HALVES)
            dve.memset(credit[:, 1:2], 0.0).then_inc(h_free, 2)
            dve.memset(credit[:, 2:3], 0.0).then_inc(comb_bc_free, RING)
            dve.memset(comb[:], 0.0).then_inc(comb_zeroed, 1)
            for i in range(2):
                dve.memset(credit[:, 3 + i:4 + i], 0.0).then_inc(y_free[i], 16)
            norm_stats(0, 0)
            norm_rstd(0, 0)
            norm(0, 0)
            split_x(0, 0)
            dve.wait_ge(small_landed, 48)
            dve.tensor_scalar(half_bw[:], bias[:, 0], 0.5, None, ALU.mult).then_inc(const_ready, 1)
            dve.wait_ge(attn_hi_ready, 1)
            dve.scalar_tensor_tensor(out=router_w[:, :, 1], in0=attn_f[:, :, RT:RT + E], scalar=WSCALE, in1=router_w[:, :, 0],
                                     op0=ALU.mult, op1=ALU.subtract).then_inc(attn_lo_ready, 1)
            for i, cols in enumerate((slice(0, WO), slice(WO, RT))):
                dve.wait_ge(attn_hi_ready, 2 + i)
                dve.scalar_tensor_tensor(out=attn_lo[:, :, cols], in0=attn_f[:, :, cols], scalar=WSCALE,
                                         in1=attn_hi[:, :, cols], op0=ALU.mult, op1=ALU.subtract).then_inc(attn_lo_ready, 1)
            dve.wait_ge(up_free, 2)
            dve.wait_ge(comb_zeroed, 1)
            for e in range(AHEAD[0]):
                split_expert(e)
            take_logits(0, 0)
            weigh(0, 0, mask(0, 0))
            for e in range(AHEAD[0], AHEAD[1]):
                split_expert(e)
            tiles(dve, step)

        @block.tensor
        def _(pe):
            def router(q, par, buf):
                pe.wait_ge(turned, count(q, par, TURN, TURN))
                for s in range(SUB):
                    terms = [(h, c) for h in range(2) for c in range(KC)]
                    for i, (h, c) in enumerate(terms):
                        last = pe.matmul(misc[:, 0, s * 2 * E:(s + 1) * 2 * E], x_t[:, buf, s, h, c],
                                         router_w[:, c, :, :].rearrange("p h e -> p (h e)"),
                                         start=(i == 0), stop=(i == len(terms) - 1))
                last.then_inc(logits_full, 1)

            def product(dst, w_hi, w_lo, x_h, x_l):
                for c in range(KC):
                    pe.matmul(dst, w_hi(c), x_h(c), start=(c == 0), stop=False)
                    pe.matmul(dst, w_hi(c), x_l(c), start=False, stop=False)
                    last = pe.matmul(dst, w_lo(c), x_h(c), start=False, stop=(c == KC - 1))
                return last

            def project(q, par):
                for i in range(3 * KC):
                    if i == 0:
                        pe.wait_ge(logits_taken, count(q, par, 1, 1))
                    elif i > 1:
                        pe.wait_ge(proj_taken, count(q, par, 3 * KC, i - 1))
                    product(misc[:, i % 2], lambda c: attn_hi[:, c, i * P:(i + 1) * P], lambda c: attn_lo[:, c, i * P:(i + 1) * P],
                            lambda c: x_t[:, par, :, 0, c], lambda c: x_t[:, par, :, 1, c]).then_inc(proj_full, 1)

            def up(q, par, e):
                n = ep(par, e)
                pe.wait_ge(up_free, count(q, par, NE, e + 1))
                for g in range(2):
                    last = product(gate_up[:, n, g],
                                   lambda c: exp_hi[:, e, c * 2 * I + g * I:c * 2 * I + (g + 1) * I],
                                   lambda c: exp_lo[:, e, c * 2 * I + g * I:c * 2 * I + (g + 1) * I],
                                   lambda c: x_t[:, par, :, 0, c], lambda c: x_t[:, par, :, 1, c])
                last.then_inc(up_full, 1)

            def add_to_acc(v_hi, v_lo, w_hi, w_lo, first=False, end=False):
                for s in range(SUB):
                    cols = slice(s * P, (s + 1) * P)
                    for i, (v, w) in enumerate(((v_hi, w_hi), (v_hi, w_lo), (v_lo, w_hi))):
                        last = pe.matmul(acc[:, s], v[:, cols], w, start=(first and i == 0 and s % 2 == 0),
                                         stop=(end and i == 2), skip_group_check=True)
                return last

            def down(q, par, e, end=False):
                n = ep(par, e)
                if e == 0:
                    pe.wait_ge(acc_free, count(q, par, HALVES, HALVES))
                pe.wait_ge(h_hi_ready, count(q, par, NE, e + 1))
                pe.wait_ge(h_lo_ready, count(q, par, NE, e + 1))
                last = add_to_acc(h_hi[:, n], h_lo[:, n], exp_hi[:, e, DOWN:DOWN + D], exp_lo[:, e, DOWN:DOWN + D],
                                  first=(e == 0), end=end)
                last.then_inc(h_free, 1)

            def recurrence_out(q, par):
                pe.wait_ge(scan_step, count(q, par, KC * SCAN_STEPS, KC * SCAN_STEPS))
                for c in range(KC):
                    add_to_acc(s_hi[:, c], s_lo[:, c], attn_hi[:, c, WO:WO + D], attn_lo[:, c, WO:WO + D])

            def step(q, par, last):
                nq, npar = q + (par == 1), 1 - par
                project(q, par)
                first = is_first(q, par)
                for e in range(NE):
                    if first:
                        pe.wait_ge(exp_lo_ready, e + 1)
                    up(q, par, e)
                    if e >= LAG:
                        down(q, par, e - LAG)
                    if last:
                        continue
                    if e == SLOT_ROUTE:
                        pe.wait_ge(proj_taken, count(q, par, 3 * KC, 3 * KC))
                        router(nq, npar, npar)
                recurrence_out(q, par)
                down(q, par, NE - 2)
                down(q, par, NE - 1, end=True)

            pe.wait_ge(attn_lo_ready, 1)
            router(0, 0, 0)
            pe.wait_ge(attn_lo_ready, 3)
            tiles(pe, step)


_OUTS = [((8, 1024, 256), 'float32')]


def kernel(L0_attn_x, L0_attn_Wp, L0_attn_bp, L0_attn_Wu, L0_attn_bu, L0_attn_Wo, L0_attn_bo, L0_ffn_input_ids,
           L0_ffn_gate_w, L0_ffn_gate_b, L0_ffn_w13, L0_ffn_w2, L0_ffn_w13_s, L0_ffn_w2_s):
    import numpy as np
    import concourse.bacc as bacc
    from concourse.bass_utils import run_bass_kernel_spmd

    def chunks(w):
        w = np.asarray(w)
        return w.reshape(w.shape[0] // P, P, w.shape[1]).transpose(1, 0, 2)

    x = np.asarray(L0_attn_x)
    d = x.shape[-1]
    attn_w = np.concatenate([chunks(np.asarray(L0_attn_Wp)[:, :2 * d]), chunks(L0_attn_Wu), chunks(L0_attn_Wo),
                             chunks(np.asarray(L0_ffn_gate_w).T)], axis=2)
    attn_b = np.concatenate([np.asarray(L0_attn_bp)[:2 * d], np.asarray(L0_attn_bu)]).reshape(3, d // P, P).transpose(2, 0, 1)
    w13 = np.concatenate([np.asarray(L0_ffn_w13), np.asarray(L0_ffn_w13_s)[None]])
    w2 = np.concatenate([np.asarray(L0_ffn_w2), np.asarray(L0_ffn_w2_s)[None]])
    ne, two_i, _ = w13.shape
    up = w13.transpose(0, 2, 1).reshape(ne, d // P, P, two_i).transpose(0, 2, 1, 3).reshape(ne, P, -1)
    expert_w = np.concatenate([up, w2.transpose(0, 2, 1)], axis=2)
    arrays = {
        "x": x.reshape(-1, d), "attn_w": attn_w, "attn_b": attn_b, "bo": np.asarray(L0_attn_bo)[None],
        "gate_b": np.asarray(L0_ffn_gate_b)[None], "expert_w": expert_w,
    }
    nc = bacc.Bacc("TRN2", target_bir_lowering=False, num_devices=1)
    args = []
    for name in arrays:
        arrays[name] = np.ascontiguousarray(arrays[name])
        args.append(nc.dram_tensor(name, arrays[name].shape, mybir.dt.from_np(arrays[name].dtype), kind="ExternalInput").ap())
    out = nc.dram_tensor("out", arrays["x"].shape, F32, kind="ExternalOutput").ap()
    scan_moe_kernel(nc, *args, out)
    r = run_bass_kernel_spmd(nc, [arrays], core_ids=[0])
    return r.results[0]["out"].reshape(x.shape)
```
